# Optimizing a Trainium2 kernel written in Bass

```python
import numpy as np
import jax
import jax.numpy as jnp

def _softmax(x, axis=-1):
    return jax.nn.softmax(x, axis=axis)

def _gelu(x):
    return jax.nn.gelu(x, approximate=True)

def _silu(x):
    return jax.nn.silu(x)

def _sigmoid(x):
    return jax.nn.sigmoid(x)

def _layernorm(x, axis=-1, eps=1e-05):
    m = jnp.mean(x, axis=axis, keepdims=True)
    v = jnp.var(x, axis=axis, keepdims=True)
    return (x - m) / jnp.sqrt(v + eps)

def _scatter_add(tgt, idx, src, axis=0):
    return tgt.at[idx].add(src)

def _segment_sum(src, seg, n):
    return jax.ops.segment_sum(src, seg, n)
kernel_name = 'mk_flamingo_gated_d1_seqx_r8_ae8b08'

def setup_inputs(seed: int=0):
    np.random.seed(seed)
    _w = jnp.asarray

    def _rec_inputs():
        import jax
        import jax.numpy as jnp
        _rk = jax.random.key(seed)
        x = -0.0002928 + 1 * jax.random.normal(jax.random.fold_in(_rk, 1), (128, 64, 128), jnp.float32)
        _lenS = 64 - jax.random.randint(jax.random.fold_in(_rk, 7), (128,), 0, max(1, 64 // 4) + 1, jnp.int32)
        _lenS2 = 64 - jax.random.randint(jax.random.fold_in(_rk, 8), (128,), 0, max(1, 64 // 4) + 1, jnp.int32)
        _ctx_1024P = jax.random.normal(jax.random.fold_in(_rk, 11), (128, 16, 128), jnp.float32)
        _ctx_1024c = jax.random.dirichlet(jax.random.fold_in(_rk, 511), 0.3 * jnp.ones((16,), jnp.float32), (128, 64))
        _ctx_1024t = jnp.einsum('bsk,bkd->bsd', _ctx_1024c, _ctx_1024P)
        _ctx_1024t = _ctx_1024t * jax.lax.rsqrt(jnp.mean(jnp.square(_ctx_1024t)) + 1e-12) * 0.953939
        ctx_1024 = -1.39393e-06 + 0.999914 * (_ctx_1024t + 0.3 * jax.random.normal(jax.random.fold_in(_rk, 611), (128, 64, 128), jnp.float32))
        _validS = jnp.arange(64)[None, :] < _lenS[:, None]
        _validS2 = jnp.arange(64)[None, :] < _lenS2[:, None]
        _causal = jnp.tril(jnp.ones((64, 64), dtype=bool))
        mask_BxS2_ik0 = jnp.where(jnp.broadcast_to(_validS2[:, :], (128, 64)), 0, 1).astype(jnp.int32)
        _g = jax.random.normal(jax.random.fold_in(_rk, 9001), (2, 1), jnp.float32)
        _g = jnp.sign(_g) * jnp.maximum(jnp.abs(_g), 1.0) + (_g == 0) * 1.0
        g_xattn = _g[0]
        g_ffn = _g[1]
        return (x, ctx_1024, mask_BxS2_ik0, g_xattn, g_ffn)
    x, ctx_1024, mask_BxS2_ik0, g_xattn, g_ffn = _rec_inputs()

    def _L0_xattn_setup():
        import jax, jax.numpy as jnp
        import numpy as np
        B, S, D, H = (2, 256, 128, 16)
        DK = D // H
        SQRT_DK = DK ** 0.5
        NEG = -1000000000.0
        key = jax.random.key(seed)
        ks = jax.random.split(key, 7)
        scale = 1.0 / np.sqrt(D)
        return {'x': jax.random.normal(ks[0], (B, S, D), jnp.float32), 'encoder_output': jax.random.normal(ks[1], (B, S, D), jnp.float32), 'mask': jax.random.randint(ks[2], (B, S), 0, 2, jnp.int32), 'WQ': jax.random.normal(ks[3], (D, D), jnp.float32) * scale, 'WK': jax.random.normal(ks[4], (D, D), jnp.float32) * scale, 'WV': jax.random.normal(ks[5], (D, D), jnp.float32) * scale, 'WO': jax.random.normal(ks[6], (D, D), jnp.float32) * scale}
    _L0_xattn_all = _L0_xattn_setup()
    _L0_xattn_in = {k: v for k, v in _L0_xattn_all.items() if k in ('WQ', 'WK', 'WV', 'WO')}
    del _L0_xattn_all

    def _L0_ffn_setup():
        import jax, jax.numpy as jnp
        import numpy as np
        DIM = 128
        INTER = 128
        E = 8
        TOPK = 2
        ROUTE_SCALE = 1.0
        SHARED_INTER = 256
        B, S = (4, 256)

        def _moe_forward(x, gate_w, gate_b, w1, b1, w3, b3, w2, b2, ws1, bs1, ws3, bs3, ws2, bs2):
            Bq, Sq, D = x.shape
            xt = x.reshape(-1, D)
            logits = (xt @ gate_w.T + gate_b).astype(jnp.float32)
            scores = jax.nn.softmax(logits, axis=-1)
            top_w, top_i = jax.lax.top_k(scores, TOPK)
            weights = (top_w * ROUTE_SCALE).astype(x.dtype)
            gate_dense = jnp.sum(jax.nn.one_hot(top_i, E, dtype=x.dtype) * weights[..., None], axis=1)

            def expert(w1e, b1e, w3e, b3e, w2e, b2e):
                h = jax.nn.silu(xt @ w1e.T + b1e) * (xt @ w3e.T + b3e)
                return h @ w2e.T + b2e
            outs = jax.vmap(expert)(w1, b1, w3, b3, w2, b2)
            y = jnp.einsum('etd,te->td', outs, gate_dense)
            z = jax.nn.silu(xt @ ws1.T + bs1) * (xt @ ws3.T + bs3) @ ws2.T + bs2
            return (y + z).reshape(Bq, Sq, D)
        key = jax.random.key(seed)
        ks = jax.random.split(key, 10)

        def w(k, shape, scale=0.02):
            return jax.random.normal(k, shape, jnp.float32) * scale
        return {'x': jax.random.normal(ks[0], (B, S, DIM), jnp.float32), 'gate_w': w(ks[1], (E, DIM)), 'gate_b': jnp.zeros((E,), jnp.float32), 'w1': w(ks[2], (E, INTER, DIM)), 'b1': jnp.zeros((E, INTER), jnp.float32), 'w3': w(ks[3], (E, INTER, DIM)), 'b3': jnp.zeros((E, INTER), jnp.float32), 'w2': w(ks[4], (E, DIM, INTER)), 'b2': jnp.zeros((E, DIM), jnp.float32), 'ws1': w(ks[5], (SHARED_INTER, DIM)), 'bs1': jnp.zeros((SHARED_INTER,), jnp.float32), 'ws3': w(ks[6], (SHARED_INTER, DIM)), 'bs3': jnp.zeros((SHARED_INTER,), jnp.float32), 'ws2': w(ks[7], (DIM, SHARED_INTER)), 'bs2': jnp.zeros((DIM,), jnp.float32)}
    _L0_ffn_all = _L0_ffn_setup()
    _L0_ffn_in = {k: v for k, v in _L0_ffn_all.items() if k in ('gate_w', 'gate_b', 'w1', 'b1', 'w3', 'b3', 'w2', 'b2', 'ws1', 'bs1', 'ws3', 'bs3', 'ws2', 'bs2')}
    del _L0_ffn_all
    return {'x': x, 'ctx_1024': ctx_1024, 'mask_BxS2_ik0': mask_BxS2_ik0, 'g_xattn': g_xattn, 'g_ffn': g_ffn, 'L0_xattn_WQ': _L0_xattn_in['WQ'], 'L0_xattn_WK': _L0_xattn_in['WK'], 'L0_xattn_WV': _L0_xattn_in['WV'], 'L0_xattn_WO': _L0_xattn_in['WO'], 'L0_ffn_gate_w': _L0_ffn_in['gate_w'], 'L0_ffn_gate_b': _L0_ffn_in['gate_b'], 'L0_ffn_w1': _L0_ffn_in['w1'], 'L0_ffn_b1': _L0_ffn_in['b1'], 'L0_ffn_w3': _L0_ffn_in['w3'], 'L0_ffn_b3': _L0_ffn_in['b3'], 'L0_ffn_w2': _L0_ffn_in['w2'], 'L0_ffn_b2': _L0_ffn_in['b2'], 'L0_ffn_ws1': _L0_ffn_in['ws1'], 'L0_ffn_bs1': _L0_ffn_in['bs1'], 'L0_ffn_ws3': _L0_ffn_in['ws3'], 'L0_ffn_bs3': _L0_ffn_in['bs3'], 'L0_ffn_ws2': _L0_ffn_in['ws2'], 'L0_ffn_bs2': _L0_ffn_in['bs2']}

def reference(x, ctx_1024, mask_BxS2_ik0, g_xattn, g_ffn, L0_xattn_WQ, L0_xattn_WK, L0_xattn_WV, L0_xattn_WO, L0_ffn_gate_w, L0_ffn_gate_b, L0_ffn_w1, L0_ffn_b1, L0_ffn_w3, L0_ffn_b3, L0_ffn_w2, L0_ffn_b2, L0_ffn_ws1, L0_ffn_bs1, L0_ffn_ws3, L0_ffn_bs3, L0_ffn_ws2, L0_ffn_bs2):
    import jax
    import jax.numpy as jnp

    def _L0_xattn_ref(x, encoder_output, mask, WQ, WK, WV, WO):
        import jax, jax.numpy as jnp
        import numpy as np
        B, S, D, H = (2, 256, 128, 16)
        DK = D // H
        SQRT_DK = DK ** 0.5
        NEG = -1000000000.0
        b, s, d = x.shape
        q = (x @ WQ).reshape(b, s, H, DK).transpose(0, 2, 1, 3)
        k = (encoder_output @ WK).reshape(b, s, H, DK).transpose(0, 2, 1, 3)
        v = (encoder_output @ WV).reshape(b, s, H, DK).transpose(0, 2, 1, 3)
        scores = jnp.einsum('bhqd,bhkd->bhqk', q, k) / SQRT_DK
        future = jnp.triu(jnp.ones((s, s), jnp.int32), 1)
        m = mask[:, None, :, None] + future[None, None, :, :]
        scores = jnp.where(m != 0, NEG, scores)
        attn = jax.nn.softmax(scores, axis=-1)
        ctx = jnp.einsum('bhqk,bhkd->bqhd', attn, v).reshape(b, s, d)
        return ctx @ WO

    def _L0_ffn_ref(x, gate_w, gate_b, w1, b1, w3, b3, w2, b2, ws1, bs1, ws3, bs3, ws2, bs2):
        import jax, jax.numpy as jnp
        import numpy as np
        DIM = 128
        INTER = 128
        E = 8
        TOPK = 2
        ROUTE_SCALE = 1.0
        SHARED_INTER = 256
        B, S = (4, 256)

        def _moe_forward(x, gate_w, gate_b, w1, b1, w3, b3, w2, b2, ws1, bs1, ws3, bs3, ws2, bs2):
            Bq, Sq, D = x.shape
            xt = x.reshape(-1, D)
            logits = (xt @ gate_w.T + gate_b).astype(jnp.float32)
            scores = jax.nn.softmax(logits, axis=-1)
            top_w, top_i = jax.lax.top_k(scores, TOPK)
            weights = (top_w * ROUTE_SCALE).astype(x.dtype)
            gate_dense = jnp.sum(jax.nn.one_hot(top_i, E, dtype=x.dtype) * weights[..., None], axis=1)

            def expert(w1e, b1e, w3e, b3e, w2e, b2e):
                h = jax.nn.silu(xt @ w1e.T + b1e) * (xt @ w3e.T + b3e)
                return h @ w2e.T + b2e
            outs = jax.vmap(expert)(w1, b1, w3, b3, w2, b2)
            y = jnp.einsum('etd,te->td', outs, gate_dense)
            z = jax.nn.silu(xt @ ws1.T + bs1) * (xt @ ws3.T + bs3) @ ws2.T + bs2
            return (y + z).reshape(Bq, Sq, D)
        return _moe_forward(x, gate_w, gate_b, w1, b1, w3, b3, w2, b2, ws1, bs1, ws3, bs3, ws2, bs2)
    x = x + jnp.tanh(g_xattn[0]) * _L0_xattn_ref(_layernorm(x, axis=-1), ctx_1024, mask_BxS2_ik0, L0_xattn_WQ, L0_xattn_WK, L0_xattn_WV, L0_xattn_WO)
    x = x + jnp.tanh(g_ffn[0]) * _L0_ffn_ref(_layernorm(x, axis=-1), L0_ffn_gate_w, L0_ffn_gate_b, L0_ffn_w1, L0_ffn_b1, L0_ffn_w3, L0_ffn_b3, L0_ffn_w2, L0_ffn_b2, L0_ffn_ws1, L0_ffn_bs1, L0_ffn_ws3, L0_ffn_bs3, L0_ffn_ws2, L0_ffn_bs2)
    return x

_drawn_inputs = setup_inputs


def setup_inputs(seed=0):
    import zlib

    import numpy as np

    out = dict(_drawn_inputs(seed))
    spreads = {'L0_ffn_gate_b': (0.0, 0.609),
     'L0_ffn_b1': (0.0, 0.8),
     'L0_ffn_b3': (0.0, 0.8),
     'L0_ffn_b2': (0.0, 0.417),
     'L0_ffn_bs1': (0.0, 0.8),
     'L0_ffn_bs3': (0.0, 0.8),
     'L0_ffn_bs2': (0.0, 0.431)}
    factors = {'L0_ffn_gate_w': 3.433,
     'L0_ffn_w1': 8.0,
     'L0_ffn_w3': 8.0,
     'L0_ffn_w2': 8.0,
     'L0_ffn_ws1': 7.084,
     'L0_ffn_ws3': 7.091,
     'L0_ffn_ws2': 6.442}
    for name, (base, spread) in spreads.items():
        noise = np.random.default_rng([zlib.crc32(name.encode()), seed]).standard_normal(out[name].shape)
        drawn = base * np.exp(spread * noise) if base else spread * noise
        out[name] = jnp.asarray(drawn.astype(out[name].dtype))
    for name, factor in factors.items():
        out[name] = (out[name] * factor).astype(out[name].dtype)
    return out
```

```python
import concourse.bass as bass
from concourse import mybir
from contextlib import ExitStack

BATCH, SEQ, DIM, HEADS = 128, 64, 128, 16
DK = DIM // HEADS
EXPERTS, INTER, TOPK, SHARED = 8, 128, 2, 256
TOKENS = BATCH * SEQ
TILE = 128
TILES = TOKENS // TILE
UT = 2
UNITS = TILES // UT
UTOK = UT * TILE
GT = 2 * UT
GROUPS = TILES // GT
NEG = -1.0e9
EPS = 1e-5
SCORE_SCALE = float(DK) ** -0.5
HG = 4
VW = 2 * 2 * DK + 2

ROW = DIM + 2
ETILE = 256
REGION = TOKENS + ETILE
SPARE = EXPERTS * REGION
ETILES = (TOPK * TOKENS // ETILE + EXPERTS - 1 + 1) // 2 * 2
SPARES = ETILES - TOPK * TOKENS // ETILE
PADS = EXPERTS + SPARES
WROW = 3 * INTER + 2
CG = 4


class At:

    def __init__(self, it, k):
        self.n = it * 2 + k
        self.half = it + k // 2
        self.par = k % 2
        self.known = isinstance(it, int)

    def exists(self):
        return (not self.known) or 0 <= self.n < UNITS

    def later_than(self, m):
        return (not self.known) or self.n >= m


class Links:

    def __init__(self, engine, sem):
        self.engine, self.sem, self.count, self.base = engine, sem, 0, 0

    def done(self, ins):
        ins.then_inc(self.sem, 1)
        self.count += 1

    def wait(self, apart=False):
        if apart:
            wait_apart(self.engine, (self.sem, self.base + self.count))
        else:
            self.engine.wait_ge(self.sem, self.base + self.count)


def wait_apart(engine, *waits):
    for s, v in waits:
        engine.wait_ge(s, v)
    engine.nop(nofuse=True)


def spread(ap, axis, n):
    wide = ap.unsqueeze(axis)
    shape = list(wide.shape)
    shape[axis] = n
    return wide.broadcast_to(shape)


def build_program(nc, x, ctx_in, mask, g_xattn, g_ffn, wq, wk, wv, wo, gate_w, gate_b, experts, b2,
                  ws1, bs1, ws3, bs3, ws2, bs2, consts, dest_rows, pad_rows, out):
    f32, bf16, i32, u32 = mybir.dt.float32, mybir.dt.bfloat16, mybir.dt.int32, mybir.dt.uint32
    ALU, ACT, AX = mybir.AluOpType, mybir.ActivationFunctionType, mybir.AxisListType

    x_tiles = x.rearrange("(a r) s d -> (r s) a d", r=2)
    ctx_tiles = ctx_in.rearrange("(a r) s d -> (r s) a d", r=2)
    out_tiles = out.rearrange("(a r) s d -> (r s) a d", r=2)
    mask_rows = mask.rearrange("(a r) s -> a (r s)", r=2)

    routed = nc.dram_tensor("routed_rows", [SPARE + SPARES * ETILE, ROW], f32, kind="Internal").ap()
    results = nc.dram_tensor("expert_results", [TOPK * TOKENS + PADS * ETILE, DIM], f32, kind="Internal").ap()

    ctx = ExitStack()
    with ctx:
        def sb(name, shape, dt=f32):
            return ctx.enter_context(nc.sbuf_tensor(name, shape, dt))

        def sem(name):
            return ctx.enter_context(nc.semaphore(name))

        X = sb("X", [128, TILES, DIM])
        X2T = sb("X2T", [128, TOKENS])
        CST = sb("CST", [128, consts.shape[1]])
        DEST = sb("DEST", [128, TOPK, TILES], i32)
        at = {}
        pos = 0
        for name, width in CONST_WIDTHS:
            at[name] = CST[:, pos:pos + width]
            pos += width
        ident, hmask, iota8, base8, tri8, iota_tiles = (
            at[n] for n in ("ident", "hmask", "iota8", "base8", "tri8", "iota_tiles"))
        I2 = sb("I2", [128, 128], bf16)
        TRI = sb("TRI", [128, 128], bf16)
        RANK = sb("RANK", [128, 128], bf16)
        ONES = sb("ONES", [128, 128], bf16)
        TG = sb("TG", [128, 2])
        NM = sb("NM", [128, TILES])
        CARRY = sb("CARRY", [128, GT + 1, EXPERTS], bf16)
        WQ, WK, WV, WO = (sb(n, [128, DIM]) for n in ("WQ", "WK", "WV", "WO"))
        GW = sb("GW", [128, EXPERTS])
        GB = sb("GB", [128, EXPERTS])
        WS1, WS3 = sb("WS1", [128, SHARED]), sb("WS3", [128, SHARED])
        WS2 = sb("WS2", [128, SHARED // 128, DIM])
        BS = sb("BS", [128, 2, SHARED // 128])
        BS2 = sb("BS2", [128, DIM])

        PS = [ctx.enter_context(nc.psum_tensor(f"PS{i}", [128, 512], f32)) for i in range(8)]

        with ExitStack() as own:
            MI = own.enter_context(nc.sbuf_tensor("MI", [TILES, TILE], i32))
            MF = own.enter_context(nc.sbuf_tensor("MF", [TILES, TILE], f32))
            G2 = own.enter_context(nc.sbuf_tensor("G2", [128, 2], f32))
            loaded, mask_float, mask_turned, setup = (sem(n) for n in ("loaded", "mask_float", "mask_turned", "setup"))
            block = own.enter_context(nc.Block())
            loads = [(CST[:, :], consts), (DEST[:, :, :], dest_rows), (MI[:, :], mask_rows),
                     (G2[:, 0:1], g_xattn.partition_broadcast(128)), (G2[:, 1:2], g_ffn.partition_broadcast(128)),
                     (WQ[:, :], wq), (WK[:, :], wk), (WV[:, :], wv), (WO[:, :], wo), (GW[:, :], gate_w),
                     (GB[:, :], gate_b.partition_broadcast(128)), (WS1[:, :], ws1), (WS3[:, :], ws3),
                     (WS2[:, :, :], ws2.rearrange("(c p) d -> p c d", p=128)),
                     (BS[:, 0, :], bs1), (BS[:, 1, :], bs3),
                     (BS2[:, :], bs2.partition_broadcast(128))]
            HALF_L = len(loads) // 2

            @block.sync
            def _(sp):
                for dst, src in loads[:HALF_L]:
                    sp.dma_start(dst, src).then_inc(loaded, 16)

            @block.scalar
            def _(act):
                for dst, src in loads[HALF_L:]:
                    act.dma_start(dst, src).then_inc(loaded, 16)
                act.wait_ge(loaded, 16 * len(loads))
                nc.scalar.activation(TG[:, :], G2[:, :], ACT.Tanh).then_inc(setup, 1)

            @block.vector
            def _(dve):
                dve.wait_ge(loaded, 16 * len(loads))
                nc.vector.tensor_scalar(MF[:, :], MI[:, :], 0.0, None, ALU.is_equal).then_inc(mask_float, 1)
                for dst, name in ((I2, "i2"), (TRI, "tri"), (RANK, "rank"), (ONES, "ones")):
                    nc.vector.tensor_copy(dst[:, :], at[name]).then_inc(setup, 1)
                nc.vector.memset(CARRY[:, :, :], 0.0).then_inc(setup, 1)
                dve.wait_ge(mask_turned, 1)
                nc.vector.tensor_copy(NM[:, :], PS[0][:, 0:TILES]).then_inc(setup, 1)

            @block.tensor
            def _(pe):
                pe.wait_ge(loaded, 16 * len(loads))
                pe.wait_ge(mask_float, 1)
                nc.tensor.transpose(PS[0][:, 0:TILES], MF[:, :], ident[0:TILES, 0:TILES]).then_inc(mask_turned, 1)

            @block.gpsimd
            def _(pool):
                pool.wait_ge(setup, 7)

        with ExitStack() as own:
            def sa(name, shape, dt=f32):
                return own.enter_context(nc.sbuf_tensor(name, shape, dt))

            C = sa("C", [128, 2, UT, DIM])
            XN = sa("XN", [128, 2, UT, DIM])
            ST1, ST2 = sa("ST1", [128, UT, 6]), sa("ST2", [128, UT, 6])
            MV1, MV2 = sa("MV1", [128, UT, 2]), sa("MV2", [128, UT, 2])
            RS1, RS2, VE1, VE2 = (sa(n, [128, UT]) for n in ("RS1", "RS2", "VE1", "VE2"))
            RM1 = sa("RM1", [128, UT])
            HALFNEG, EPSV = sa("HALFNEG", [128, UT]), sa("EPSV", [128, UT])
            XCT = sa("XCT", [128, 2, UTOK])
            QB = sa("QB", [128, 2 * UT, HG, SEQ])
            KT = sa("KT", [128, UTOK])
            MP = sa("MP", [128, 2, UT, TILE], bf16)
            MX = sa("MX", [128, HG, 8])
            P = sa("P", [128, 2, HG, 512])
            PT = sa("PT", [128, 2, 512])
            VX = sa("VX", [128, 2, UT, HEADS // 2, VW])
            O = sa("O", [128, UT, 2, 4, VW])
            R = sa("R", [128, UT * 8, 2])
            A = sa("A", [128, UT, DIM])
            AT = sa("AT", [128, UTOK])
            X2 = sa("X2", [128, GT, DIM])
            X2G = sa("X2G", [128, GT * TILE])
            LG = sa("LG", [128, GT, EXPERTS])
            M8 = sa("M8", [128, GT, 8])
            I8 = sa("I8", [128, GT, 8], u32)
            IF = sa("IF", [128, GT, TOPK])
            OH = sa("OH", [128, GT, TOPK, EXPERTS])
            OHS = sa("OHS", [128, GT, EXPERTS], bf16)
            NL = sa("NL", [128, GT, EXPERTS + TOPK])
            EX = sa("EX", [128, GT, EXPERTS + TOPK])
            Z, RZ = sa("Z", [128, GT]), sa("RZ", [128, GT])
            RB = sa("RB", [128, GT, EXPERTS])
            OP = sa("OP", [128, GT, TOPK, EXPERTS])
            PF = sa("PF", [128, GT, TOPK])
            IDX = sa("IDX", [128, TOPK, GT], i32)
            STAGE = sa("STAGE", [128, TOPK, GT, ROW])

            S, T, M0, M1 = PS[0:4], PS[4:6], PS[6], PS[7]

            x_in = [sem("x_in0"), sem("x_in1")]
            c_in = [sem("c_in0"), sem("c_in1")]
            (consts_a, stat1, xn_done, mp_done, xc_ready, xc_out, qk_ready, q_out, k_out, v_ready, v_out, s_ready,
             sub_done, exp_done, t_ready, pt_out, pva_ready, pva_out, pvb_ready, pvb_out, norm_done, at_ready, at_out,
             wo_ready, resid, stat2, rs2_done, xn2_done, x2t_ready, x2t_out, x2t_saved, logits_ready, logits_used,
             nl_done, e_done, w_done, oh_done, rank_ready, rank_used, idx_done, stage_x, stage_dest, scattered,
             dve_own, pool_own) = (sem(n) for n in (
                 "consts_a", "stat1", "xn_done", "mp_done", "xc_ready", "xc_out", "qk_ready", "q_out", "k_out",
                 "v_ready", "v_out", "s_ready", "sub_done", "exp_done", "t_ready", "pt_out", "pva_ready", "pva_out",
                 "pvb_ready", "pvb_out", "norm_done", "at_ready", "at_out", "wo_ready", "resid", "stat2", "rs2_done",
                 "xn2_done", "x2t_ready", "x2t_out", "x2t_saved", "logits_ready", "logits_used", "nl_done", "e_done",
                 "w_done", "oh_done", "rank_ready", "rank_used", "idx_done", "stage_x", "stage_dest", "scattered",
                 "dve_own", "pool_own"))

            block = own.enter_context(nc.Block())

            def around(it, k):
                return At(it, k + 2), At(it, k + 1), At(it, k), At(it, k - 1), At(it, k - 2)

            TRIPS = (UNITS - 6) // 2
            BEFORE = [(0, -2), (0, -1), (0, 0), (0, 1), (0, 2), (0, 3)]
            AFTER = [(TRIPS, 2), (TRIPS, 3), (TRIPS, 4), (TRIPS, 5), (TRIPS, 6), (TRIPS, 7)]

            def run(engine, step, links=None, per_trip=0):
                for it, k in BEFORE:
                    step(it, k)
                first = links.count if links else 0
                with engine.Fori(1, TRIPS) as it:
                    if links:
                        links.base, links.count = first + (it - 1) * per_trip, 0
                    step(it, 2)
                    step(it, 3)
                    if links:
                        assert links.count == per_trip, (links.count, per_trip)
                if links:
                    links.base, links.count = 0, first + (TRIPS - 1) * per_trip
                for it, k in AFTER:
                    step(it, k)

            def tiles_of(u):
                return bass.ds(u.n * UT, UT)

            @block.sync
            def _(sp):
                def load_x(u):
                    sp.dma_start(X[:, tiles_of(u), :], x_tiles[:, tiles_of(u), :]).then_inc(x_in[u.par], 16)

                def load_c(u):
                    sp.dma_start(C[:, u.par, :, :], ctx_tiles[:, tiles_of(u), :]).then_inc(c_in[u.par], 16)

                load_x(At(0, 0))
                load_c(At(0, 0))
                load_x(At(0, 1))
                load_c(At(0, 1))

                def step(it, k):
                    e, f, i, u, w = around(it, k)
                    f2 = At(it, k + 3)
                    if f2.exists() and f2.later_than(2):
                        sp.wait_ge(x_in[f.par], 16 * (f.half + 1))
                        load_x(f2)
                    if f2.exists() and f2.later_than(2):
                        sp.wait_ge(xc_ready, f.n + 1)
                        load_c(f2)
                    if w.exists() and w.par:
                        sp.wait_ge(x2t_out, w.n + 1)
                        sp.dma_start(X2T[:, bass.ds(w.half * (GT * TILE), GT * TILE)], X2G[:, :]).then_inc(x2t_saved, 16)

                run(sp, step)
                sp.wait_ge(x2t_saved, 16 * GROUPS)

            @block.tensor
            def _(pe):
                pe.wait_ge(consts_a, 3)

                def scores(i, t):
                    for b in range(2):
                        col = t * TILE + b * SEQ
                        for jp in range(2):
                            for g in range(HG):
                                rows = slice(32 * g, 32 * g + 32)
                                o = ((t * 2 + jp) * 2 + b) * SEQ
                                last = nc.tensor.matmul(
                                    S[g][:, o:o + SEQ], QB[rows, 2 * t + b, 2 * jp:2 * jp + 2, :], KT[rows, col:col + SEQ],
                                    start=False, stop=(t == 1 and b == 1 and jp == 1), tile_position=(32 * g, 0),
                                    skip_group_check=True)
                    return last

                def turn_p(u, g):
                    if u.later_than(1) or g >= 2:
                        pe.wait_ge(pt_out, u.n * 4 + g - 1)
                    for c in range(4):
                        last = nc.tensor.transpose(T[g % 2][:, 128 * c:128 * c + 128],
                                                   P[:, u.par, g, 128 * c:128 * c + 128], ident)
                    last.then_inc(t_ready, 1)

                def p_v(u, g):
                    pe.wait_ge(pt_out, u.n * 4 + g + 1)
                    for t in range(UT):
                        for jp in range(2):
                            o = (t * 4 + (g % 2) * 2 + jp) * VW
                            last = nc.tensor.matmul(M0[:, o:o + VW], PT[:, g % 2, (2 * t + jp) * 128:(2 * t + jp) * 128 + 128],
                                                    VX[:, u.par, t, 2 * g + jp, :], start=True, stop=True)
                    return last

                def step(it, k):
                    e, f, i, u, w = around(it, k)
                    routing = w.exists() and w.par
                    if w.exists():
                        pe.wait_ge(norm_done, w.n + 1)
                        for t in range(UT):
                            last = nc.tensor.transpose(M0[:, t * TILE:(t + 1) * TILE], A[:, t, :], ident)
                        last.then_inc(at_ready, 1)
                    if i.exists():
                        pe.wait_ge(q_out, i.n + 1)
                        pe.wait_ge(k_out, i.n + 1)
                        pe.wait_ge(mp_done, i.n + 1)
                        if i.later_than(1):
                            pe.wait_ge(sub_done, i.n * HG)
                        for g in range(HG):
                            m = spread(MP[:, i.par, :, :], 2, 2)
                            nc.tensor.matmul(S[g][:, :], I2[:, :], m, start=True, stop=False, skip_group_check=True)
                        scores(i, 0)
                    if w.exists():
                        pe.wait_ge(at_out, w.n + 1)
                        if i.exists():
                            pe.wait_ge(v_out, 2 * (i.n + 1))
                        if w.later_than(2) and not w.par:
                            pe.wait_ge(rank_used, w.half)
                        for t in range(UT):
                            last = nc.tensor.matmul(M1[:, t * DIM:(t + 1) * DIM], AT[:, t * TILE:(t + 1) * TILE], WO[:, :],
                                                    start=True, stop=True)
                        last.then_inc(wo_ready, 1)
                    if i.exists():
                        scores(i, 1).then_inc(s_ready, 1)
                    if f.exists():
                        pe.wait_ge(xn_done, f.n + 1)
                        pe.wait_ge(c_in[f.par], 16 * (f.half + 1))
                        if w.exists():
                            pe.wait_ge(at_out, w.n + 1)
                        for t in range(UT):
                            nc.tensor.transpose(M0[:, t * TILE:(t + 1) * TILE], XN[:, f.par, t, :], ident)
                        for t in range(UT):
                            last = nc.tensor.transpose(M0[:, UTOK + t * TILE:UTOK + (t + 1) * TILE], C[:, f.par, t, :], ident)
                        last.then_inc(xc_ready, 1)
                    if u.exists():
                        pe.wait_ge(exp_done, (u.n + 1) * 2)
                        turn_p(u, 0)
                        turn_p(u, 1)
                    if w.exists():
                        pe.wait_ge(xn2_done, w.n + 1)
                        for t in range(UT):
                            last = nc.tensor.transpose(M1[:, t * TILE:(t + 1) * TILE], X2[:, w.par * UT + t, :], ident)
                        last.then_inc(x2t_ready, 1)
                    if u.exists():
                        if f.exists():
                            pe.wait_ge(xc_out, f.n + 1)
                        p_v(u, 0)
                        turn_p(u, 2)
                        p_v(u, 1).then_inc(pva_ready, 1)
                    if routing:
                        pe.wait_ge(x2t_out, w.n + 1)
                        for t in range(GT):
                            last = nc.tensor.matmul(M1[:, t * EXPERTS:(t + 1) * EXPERTS], X2G[:, t * TILE:(t + 1) * TILE],
                                                    GW[:, :], start=True, stop=True)
                        last.then_inc(logits_ready, 1)
                    if u.exists():
                        turn_p(u, 3)
                    if f.exists():
                        pe.wait_ge(xc_out, f.n + 1)
                        if routing:
                            pe.wait_ge(logits_used, w.half + 1)
                        elif w.exists():
                            pe.wait_ge(x2t_out, w.n + 1)
                        elif f.later_than(1):
                            pe.wait_ge(v_out, 2 * f.n)
                        nc.tensor.matmul(M1[:, 0:UTOK], WQ[:, :], XCT[:, 0, :], start=True, stop=True)
                        nc.tensor.matmul(M1[:, UTOK:2 * UTOK], WK[:, :], XCT[:, 1, :], start=True, stop=True).then_inc(qk_ready, 1)
                    if u.exists():
                        pe.wait_ge(pva_out, u.n + 1)
                        p_v(u, 2)
                        p_v(u, 3).then_inc(pvb_ready, 1)
                    if routing:
                        pe.wait_ge(oh_done, w.half + 1)
                        if f.exists():
                            pe.wait_ge(q_out, f.n + 1)
                            pe.wait_ge(k_out, f.n + 1)
                        nc.tensor.matmul(M1[:, 0:GT * EXPERTS], RANK[:, :], OHS[:, :, :], start=True, stop=False)
                        nc.tensor.matmul(M1[:, 0:GT * EXPERTS], ONES[:, :], CARRY[:, 0:GT, :], start=False,
                                         stop=True).then_inc(rank_ready, 1)
                    if f.exists():
                        if routing:
                            pe.wait_ge(rank_used, w.half + 1)
                        pe.wait_ge(q_out, f.n + 1)
                        pe.wait_ge(k_out, f.n + 1)
                        for t in range(UT):
                            last = nc.tensor.matmul(M1[:, t * DIM:(t + 1) * DIM], XCT[:, 1, t * TILE:(t + 1) * TILE], WV[:, :],
                                                    start=True, stop=True)
                        last.then_inc(v_ready, 1)

                run(pe, step)

            @block.scalar
            def _(act):
                def copy(dst, src):
                    return nc.scalar.activation(dst, src, ACT.Copy)

                def p_out(u, g):
                    act.wait_ge(t_ready, u.n * 4 + g + 1)
                    copy(PT[:, g % 2, :], T[g % 2][:, :]).then_inc(pt_out, 1)

                def step(it, k):
                    e, f, i, u, w = around(it, k)
                    routing = w.exists() and w.par
                    if w.exists():
                        act.wait_ge(at_ready, w.n + 1)
                        copy(AT[:, :], M0[:, 0:UTOK]).then_inc(at_out, 1)
                    if f.exists():
                        act.wait_ge(xc_ready, f.n + 1)
                        copy(XCT[:, :, :], M0[:, :]).then_inc(xc_out, 1)
                    if u.exists():
                        p_out(u, 0)
                        p_out(u, 1)
                    if w.exists():
                        act.wait_ge(x2t_ready, w.n + 1)
                        if not w.par and w.later_than(2):
                            act.wait_ge(x2t_saved, 16 * w.half)
                        copy(X2G[:, w.par * UTOK:(w.par + 1) * UTOK], M1[:, 0:UTOK]).then_inc(x2t_out, 1)
                    if u.exists():
                        p_out(u, 2)
                        act.wait_ge(pva_ready, u.n + 1)
                        if u.later_than(1):
                            act.wait_ge(norm_done, u.n)
                        copy(O[:, :, 0, :, :], M0[:, 0:UT * 4 * VW]).then_inc(pva_out, 1)
                    if u.exists():
                        p_out(u, 3)
                    if f.exists():
                        act.wait_ge(qk_ready, f.n + 1)
                        copy(KT[:, :], M1[:, UTOK:2 * UTOK]).then_inc(k_out, 1)
                    if routing:
                        act.wait_ge(nl_done, w.half + 1)
                        nc.scalar.activation(EX[:, :, :], NL[:, :, :], ACT.Exp).then_inc(e_done, 1)
                    if u.exists():
                        act.wait_ge(pvb_ready, u.n + 1)
                        copy(O[:, :, 1, :, :], M0[:, 0:UT * 4 * VW]).then_inc(pvb_out, 1)
                    if f.exists():
                        act.wait_ge(v_ready, f.n + 1)
                        for b in range(2):
                            rows = slice(SEQ * b, SEQ * b + SEQ)
                            copy(VX[rows, f.par, :, :, 16 * b:16 * b + 16],
                                 M1[rows, 0:UT * DIM].rearrange("p (t h c) -> p t h c", t=UT, c=16)).then_inc(v_out, 1)
                    if i.exists():
                        for c in range(2):
                            act.wait_ge(sub_done, i.n * HG + 2 * c + 2)
                            nc.scalar.activation(P[:, i.par, 2 * c:2 * c + 2, :], P[:, i.par, 2 * c:2 * c + 2, :], ACT.Exp,
                                                 scale=SCORE_SCALE).then_inc(exp_done, 1)
                    if routing:
                        act.wait_ge(xn2_done, w.n + 1)
                        if w.later_than(2):
                            act.wait_ge(scattered, 16 * TOPK * GT * w.half)
                        copy(STAGE[:, :, :, 0:DIM], spread(X2[:, :, :], 1, TOPK)).then_inc(stage_x, 1)

                run(act, step)

            @block.vector
            def _(dve):
                own_v = Links(dve, dve_own)
                for p in range(2):
                    own_v.done(nc.vector.memset(VX[:, p, :, :, :], 0.0))
                own_v.wait()
                for b in range(2):
                    for p in range(2):
                        ins = nc.vector.memset(VX[SEQ * b:SEQ * b + SEQ, p, :, :, 32 + b:33 + b], 1.0)
                        if p == 1:
                            ins.then_inc(consts_a, 1)
                        else:
                            own_v.done(ins)
                own_v.wait()
                nc.vector.memset(EPSV[:, :], EPS)
                nc.vector.memset(HALFNEG[:, :], -0.5).then_inc(consts_a, 1)

                def statistics(rows, st, mv, done):
                    for t in range(UT):
                        last = nc.vector.bn_stats(st[:, t, :], rows[t])
                    own_v.done(last)
                    own_v.wait(apart=True)
                    for t in range(UT):
                        last = nc.vector.bn_aggr(mv[:, t, :], st[:, t, :])
                    last.then_inc(done, 1)

                def choose(w):
                    g1 = w.half + 1
                    dve.wait_ge(logits_ready, g1)
                    nc.vector.tensor_tensor(LG[:, :, :], M1[:, 0:GT * EXPERTS].rearrange("p (t e) -> p t e", t=GT),
                                            spread(GB[:, :], 1, GT), ALU.add).then_inc(logits_used, 1)
                    wait_apart(dve, (logits_used, g1))
                    for t in range(GT):
                        ins = nc.vector.max(M8[:, t, :], LG[:, t, :])
                    own_v.done(ins)
                    own_v.wait()
                    nc.vector.tensor_tensor(NL[:, :, 0:EXPERTS], LG[:, :, :], M8[:, :, 0:1].broadcast_to([128, GT, EXPERTS]),
                                            ALU.subtract)
                    nc.vector.tensor_tensor(NL[:, :, EXPERTS:], M8[:, :, 0:TOPK], M8[:, :, 0:1].broadcast_to([128, GT, TOPK]),
                                            ALU.subtract).then_inc(nl_done, 1)
                    for t in range(GT):
                        ins = nc.vector.max_index(I8[:, t, :], M8[:, t, :], LG[:, t, :])
                    own_v.done(ins)
                    own_v.wait()
                    own_v.done(nc.vector.tensor_copy(IF[:, :, :], I8[:, :, 0:TOPK]))
                    own_v.wait()
                    own_v.done(nc.vector.tensor_tensor(OH[:, :, :, :], spread(spread(iota8, 1, TOPK), 1, GT),
                                                       spread(IF[:, :, :], 3, EXPERTS), ALU.is_equal))
                    own_v.wait()
                    own_v.done(nc.vector.tensor_tensor(OHS[:, :, :], OH[:, :, 0, :], OH[:, :, 1, :], ALU.add))
                    own_v.wait()
                    for t in range(GT):
                        ins = nc.vector.tensor_tensor(CARRY[:, t + 1, :], CARRY[:, t, :], OHS[:, t, :], ALU.add)
                        if t < GT - 1:
                            own_v.done(ins)
                            own_v.wait()
                    ins.then_inc(oh_done, 1)

                def place(w):
                    g1 = w.half + 1
                    dve.wait_ge(e_done, g1)
                    own_v.done(nc.vector.reduce_sum(Z[:, :], EX[:, :, 0:EXPERTS], AX.X))
                    own_v.wait()
                    own_v.done(nc.vector.reciprocal(RZ[:, :], Z[:, :]))
                    own_v.wait()
                    if w.later_than(2):
                        dve.wait_ge(scattered, 16 * TOPK * GT * w.half)
                    nc.vector.scalar_tensor_tensor(
                        out=STAGE[:, :, :, DIM].rearrange("p s t -> p t s"), in0=EX[:, :, EXPERTS:], scalar=TG[:, 1:2],
                        in1=spread(RZ[:, :], 2, TOPK), op0=ALU.mult, op1=ALU.mult).then_inc(w_done, 1)
                    dve.wait_ge(rank_ready, g1)
                    nc.vector.tensor_tensor(RB[:, :, :], M1[:, 0:GT * EXPERTS].rearrange("p (t e) -> p t e", t=GT),
                                            spread(base8, 1, GT), ALU.add).then_inc(rank_used, 1)
                    own_v.done(nc.vector.tensor_copy(CARRY[:, 0, :], CARRY[:, GT, :]))
                    dve.wait_ge(rank_used, g1)
                    own_v.done(nc.vector.tensor_tensor(OP[:, :, :, :], OH[:, :, :, :], spread(RB[:, :, :], 2, TOPK), ALU.mult))
                    own_v.wait()
                    own_v.done(nc.vector.reduce_sum(PF[:, :, :], OP[:, :, :, :], AX.X))
                    own_v.wait()
                    nc.vector.tensor_copy(IDX[:, :, :].rearrange("p s t -> p t s"), PF[:, :, :]).then_inc(idx_done, 1)

                def step(it, k):
                    e, f, i, u, w = around(it, k)
                    routing = w.exists() and w.par
                    if e.exists():
                        wait_apart(dve, (x_in[e.par], 16 * (e.half + 1)), *[(xn_done, e.n)] * e.later_than(1))
                        statistics([X[:, bass.ds(e.n * UT + t, 1), :] for t in range(UT)], ST1, MV1, stat1)
                    if w.exists():
                        dve.wait_ge(wo_ready, w.n + 1)
                        here = X[:, tiles_of(w), :]
                        nc.vector.scalar_tensor_tensor(
                            out=here, in0=M1[:, 0:UT * DIM].rearrange("p (t d) -> p t d", t=UT), scalar=TG[:, 0:1], in1=here,
                            op0=ALU.mult, op1=ALU.add).then_inc(resid, 1)
                        wait_apart(dve, (resid, w.n + 1))
                        statistics([X[:, bass.ds(w.n * UT + t, 1), :] for t in range(UT)], ST2, MV2, stat2)

                    def softmax_shift(g):
                        bank = S[g][:, :].rearrange("p (c k) -> p c k", c=8)
                        own_v.done(nc.vector.tensor_reduce(out=MX[:, g, :], in_=bank, axis=AX.X, op=ALU.max))
                        own_v.wait()
                        nc.vector.tensor_tensor(P[:, i.par, g, :].rearrange("p (c k) -> p c k", c=8), bank,
                                                spread(MX[:, g, :], 2, SEQ), ALU.subtract).then_inc(sub_done, 1)

                    if i.exists():
                        dve.wait_ge(s_ready, i.n + 1)
                        softmax_shift(0)
                    if w.exists():
                        dve.wait_ge(rs2_done, w.n + 1)
                        if not w.par and w.later_than(2):
                            dve.wait_ge(stage_x, w.half)
                            dve.wait_ge(x2t_ready, w.n)
                        for t in range(UT):
                            ins = nc.vector.tensor_scalar(
                                X2[:, w.par * UT + t, :], X[:, bass.ds(w.n * UT + t, 1), :], MV2[:, t, 0:1], RS2[:, t:t + 1],
                                ALU.subtract, ALU.mult)
                        ins.then_inc(xn2_done, 1)
                    if i.exists():
                        for g in range(1, HG):
                            softmax_shift(g)
                    if routing:
                        choose(w)
                    if f.exists():
                        dve.wait_ge(k_out, f.n + 1)
                        qt = M1[:, 0:UTOK].rearrange("p (s q) -> p s q", q=SEQ)
                        nc.vector.tensor_tensor(QB[:, :, :, :], spread(qt, 2, HG), spread(spread(hmask, 1, 2 * UT), 3, SEQ),
                                                ALU.mult).then_inc(q_out, 1)
                    if u.exists():
                        dve.wait_ge(pvb_out, u.n + 1)
                        if u.later_than(1):
                            dve.wait_ge(at_ready, u.n)
                        heads = O[:, :, :, :, :].rearrange("p t g c v -> p (t g c) v")
                        own_v.done(nc.vector.reciprocal(R[:, :, :], heads[:, :, 32:34]))
                        own_v.wait()
                        rows_a = A[:, :, :].rearrange("p t (h c) -> p (t h) c", c=16)
                        for b in range(2):
                            for j in range(2):
                                src = slice(SEQ * j, SEQ * j + SEQ)
                                ins = nc.vector.tensor_tensor(
                                    rows_a[SEQ * b:SEQ * b + SEQ, :, DK * j:DK * j + DK],
                                    heads[src, :, 16 * b + DK * j:16 * b + DK * j + DK],
                                    spread(R[src, :, b], 2, DK), ALU.mult)
                        ins.then_inc(norm_done, 1)
                    if routing:
                        place(w)

                run(dve, step, own_v, DVE_LINKS)

            @block.gpsimd
            def _(pool):
                own_p = Links(pool, pool_own)
                pool.wait_ge(consts_a, 3)

                def rstd(rs, ve, mv):
                    own_p.done(nc.gpsimd.tensor_tensor(ve[:, :], mv[:, :, 1], EPSV[:, :], ALU.add))
                    own_p.wait()
                    return nc.gpsimd.tensor_tensor(rs[:, :], ve[:, :], HALFNEG[:, :], ALU.pow)

                def step(it, k):
                    e, f, i, u, w = around(it, k)
                    if e.exists():
                        pool.wait_ge(stat1, e.n + 1)
                        own_p.done(rstd(RS1, VE1, MV1))
                        own_p.wait(apart=True)
                        own_p.done(nc.gpsimd.tensor_tensor(RM1[:, :], RS1[:, :], NM[:, tiles_of(e)], ALU.mult))
                        xn = XN[:, e.par, :, :]
                        own_p.done(nc.gpsimd.tensor_tensor(xn, X[:, tiles_of(e), :], spread(MV1[:, :, 0], 2, DIM), ALU.subtract))
                        own_p.wait()
                        ins = nc.gpsimd.tensor_tensor(xn, xn, spread(RM1[:, :], 2, DIM), ALU.mult)
                        ins.then_inc(xn_done, 1)
                    if w.exists():
                        pool.wait_ge(stat2, w.n + 1)
                        rstd(RS2, VE2, MV2).then_inc(rs2_done, 1)
                    if f.exists():
                        wait_apart(pool, *[(s_ready, f.n - 1)] * f.later_than(2))
                        ins = nc.gpsimd.tensor_tensor(MP[:, f.par, :, :], spread(TRI[:, :], 1, UT), spread(NM[:, tiles_of(f)], 2, TILE),
                                                      ALU.mult)
                        ins.then_inc(mp_done, 1)
                    if w.exists() and w.par:
                        if w.later_than(2):
                            pool.wait_ge(scattered, 16 * TOPK * GT * w.half)
                        nc.gpsimd.tensor_copy(STAGE[:, :, :, DIM + 1].bitcast(i32), DEST[:, :, bass.ds(w.half * GT, GT)]).then_inc(stage_dest, 1)
                        wait_apart(pool, (stage_dest, w.half + 1), (stage_x, w.half + 1), (w_done, w.half + 1),
                                   (idx_done, w.half + 1))
                        for s in range(TOPK):
                            for t in range(GT):
                                nc.gpsimd.indirect_dma_start(
                                    routed[:, :], bass.IndirectOffsetOnAxis(ap=IDX[:, s, t:t + 1], axis=0),
                                    STAGE[:, s, t, :], None).then_inc(scattered, 16)

                run(pool, step, own_p, POOL_LINKS)
                pool.wait_ge(scattered, 16 * TOPK * GT * GROUPS)

        with ExitStack() as own:
            def sa(name, shape, dt=f32):
                return own.enter_context(nc.sbuf_tensor(name, shape, dt))

            CNT, CI, NTI, NTF = sa("CNT", [1, EXPERTS]), sa("CI", [1, EXPERTS], i32), sa("NTI", [1, EXPERTS], i32), sa("NTF", [1, EXPERTS])
            CUM8, INC, SKIP = sa("CUM8", [1, EXPERTS, EXPERTS]), sa("INC", [1, EXPERTS]), sa("SKIP", [1, EXPERTS])
            PAST = sa("PAST", [1, ETILES, EXPERTS])
            PSKIP = sa("PSKIP", [1, ETILES, EXPERTS])
            EOF = sa("EOF", [1, ETILES])
            ROF, RO2 = sa("ROF", [1, ETILES]), sa("RO2", [1, ETILES])
            META = sa("META", [1, 2, ETILES], i32)
            XB = sa("XB", [128, 2, 2, ROW])
            WB = sa("WB", [128, 2, WROW])
            B2B = sa("B2B", [128, 2, DIM])
            XTB = sa("XTB", [128, 2, ETILE])
            SG = sa("SG", [128, 2, ETILE])
            HT = sa("HT", [128, 2, ETILE])
            YB = sa("YB", [128, 2, 2, DIM])
            YW = sa("YW", [128, 2, 2, DIM])
            SGS = sa("SGS", [128, 2, UTOK])
            HS = sa("HS", [128, 2, UTOK])
            ZB = sa("ZB", [128, UT, DIM])
            TX, H, SH, ZP, YP = PS[0], PS[1:3], PS[3:5], PS[5], PS[6]

            tile_in = [sem("tile_in0"), sem("tile_in1")]
            sent = [sem("sent0"), sem("sent1")]
            (count_ready, meta_done, padded, tx_ready, tx_out, h_ready, sg_done, ht_done, y_ready, yb_done, yw_done,
             sh_ready, sgs_done, hs_done, z_ready, zb_done, x_done, meta_own) = (sem(n) for n in (
                 "count_ready", "meta_done", "padded", "tx_ready", "tx_out", "h_ready", "sg_done", "ht_done", "y_ready",
                 "yb_done", "yw_done", "sh_ready", "sgs_done", "hs_done", "z_ready", "zb_done", "x_done", "meta_own"))
            block = own.enter_context(nc.Block())
            BODIES = ETILES // 2

            def run_b(engine, body):
                body(0, True, True)
                with engine.Fori(1, UNITS) as it:
                    body(it, True, False)
                with engine.Fori(UNITS, BODIES) as it:
                    body(it, False, False)

            @block.sync
            def _(sp):
                sp.wait_ge(meta_done, 1)
                for e in range(EXPERTS):
                    count = sp.value_load(CI[0:1, e:e + 1], min_val=0, max_val=TOKENS)
                    sp.dma_start(routed[bass.ds(count + e * REGION, ETILE), :], pad_rows[e * ETILE:(e + 1) * ETILE, :]).then_inc(padded, 16)
                sp.dma_start(routed[SPARE:, :], pad_rows[EXPERTS * ETILE:, :]).then_inc(padded, 16)
                sp.wait_ge(padded, 16 * (EXPERTS + 1))

                def body(it, shared, first):
                    for p in range(2):
                        n = it * 2 + p
                        if not first:
                            sp.wait_ge(sent[p], 32 * it)
                            sp.wait_ge(yb_done, 2 * it - 1 + p)
                        row = sp.value_load(META[0:1, 0, bass.ds(n, 1)], min_val=0, max_val=SPARE + (SPARES - 1) * ETILE)
                        expert = sp.value_load(META[0:1, 1, bass.ds(n, 1)], min_val=0, max_val=EXPERTS - 1)
                        sp.dma_start(XB[:, p, :, :], routed[bass.ds(row, ETILE), :].rearrange("(a p) c -> p a c", p=128)).then_inc(tile_in[p], 16)
                        sp.dma_start(WB[:, p, :], experts[bass.ds(expert * 128, 128), :]).then_inc(tile_in[p], 16)
                        sp.dma_start(B2B[:, p, :], b2[bass.ds(expert, 1), :].broadcast_to([128, DIM])).then_inc(tile_in[p], 16)

                run_b(sp, body)

            @block.tensor
            def _(pe):
                nc.tensor.matmul(PS[7][:, 0:EXPERTS], ONES[:, :], CARRY[:, 0, :], start=True, stop=True).then_inc(count_ready, 1)

                def body(it, shared, first):
                    for p in range(2):
                        pe.wait_ge(tile_in[p], 48 * (it + 1))
                        for a in range(2):
                            last = nc.tensor.transpose(TX[:, p * ETILE + a * 128:p * ETILE + a * 128 + 128], XB[:, p, a, 0:DIM], ident)
                    last.then_inc(tx_ready, 1)
                    if shared:
                        cols = X2T[:, bass.ds(it * UTOK, UTOK)]
                        for c in range(2):
                            nc.tensor.matmul(SH[0][:, c * UTOK:(c + 1) * UTOK], WS1[:, c * 128:c * 128 + 128], cols, start=True, stop=True)
                        for c in range(2):
                            last = nc.tensor.matmul(SH[1][:, c * UTOK:(c + 1) * UTOK], WS3[:, c * 128:c * 128 + 128], cols,
                                                    start=True, stop=True)
                        last.then_inc(sh_ready, 1)
                    pe.wait_ge(tx_out, it + 1)
                    for p in range(2):
                        nc.tensor.matmul(H[p][:, 0:ETILE], WB[:, p, 0:128], XTB[:, p, :], start=True, stop=True)
                        nc.tensor.matmul(H[p][:, ETILE:2 * ETILE], WB[:, p, 128:256], XTB[:, p, :], start=True, stop=True).then_inc(h_ready, 1)
                    if shared:
                        pe.wait_ge(hs_done, 2 * (it + 1))
                        if not first:
                            pe.wait_ge(zb_done, it)
                        for t in range(UT):
                            for c in range(2):
                                last = nc.tensor.matmul(ZP[:, t * DIM:(t + 1) * DIM], HS[:, c, t * TILE:(t + 1) * TILE], WS2[:, c, :],
                                                        start=(c == 0), stop=(c == 1))
                        last.then_inc(z_ready, 1)
                    for p in range(2):
                        pe.wait_ge(ht_done, it * 2 + p + 1)
                        if not first:
                            pe.wait_ge(yb_done, it * 2)
                        for a in range(2):
                            last = nc.tensor.matmul((YP if p == 0 else PS[7])[:, a * DIM:(a + 1) * DIM], HT[:, p, a * 128:a * 128 + 128],
                                                    WB[:, p, 256:384], start=True, stop=True)
                        last.then_inc(y_ready, 1)

                run_b(pe, body)

            @block.scalar
            def _(act):
                def body(it, shared, first):
                    if shared:
                        act.wait_ge(sh_ready, it + 1)
                        if not first:
                            act.wait_ge(hs_done, 2 * it)
                        for c in range(2):
                            nc.scalar.activation(SGS[:, c, :], SH[0][:, c * UTOK:(c + 1) * UTOK], ACT.Silu,
                                                 bias=BS[:, 0, c:c + 1]).then_inc(sgs_done, 1)
                    for p in range(2):
                        act.wait_ge(h_ready, it * 2 + p + 1)
                        if not first:
                            act.wait_ge(ht_done, it * 2)
                        nc.scalar.activation(SG[:, p, :], H[p][:, 0:ETILE], ACT.Silu, bias=WB[:, p, 384:385]).then_inc(sg_done, 1)
                    for p in range(2):
                        act.wait_ge(yb_done, it * 2 + p + 1)
                        if not first:
                            act.wait_ge(sent[p], 32 * it)
                        for a in range(2):
                            nc.scalar.activation(YW[:, p, a, :], YB[:, p, a, :], ACT.Copy,
                                                 scale=XB[:, p, a, DIM:DIM + 1]).then_inc(yw_done, 1)

                run_b(act, body)

            @block.vector
            def _(dve):
                own_v = Links(dve, meta_own)

                def chain(ins):
                    own_v.done(ins)
                    own_v.wait()

                dve.wait_ge(count_ready, 1)
                chain(nc.vector.tensor_copy(CI[:, :], PS[7][0:1, 0:EXPERTS]))
                chain(nc.vector.tensor_scalar(NTI[:, :], CI[:, :], float(ETILE - 1), None, ALU.add))
                chain(nc.vector.tensor_scalar(NTI[:, :], NTI[:, :], ETILE.bit_length() - 1, None, ALU.arith_shift_right))
                chain(nc.vector.tensor_copy(NTF[:, :], NTI[:, :]))
                chain(nc.vector.tensor_tensor(CUM8[:, :, :], spread(NTF[:, :], 1, EXPERTS),
                                              tri8[0:1, :].rearrange("p (a b) -> p a b", a=EXPERTS), ALU.mult))
                chain(nc.vector.reduce_sum(INC[:, :], CUM8[:, :, :], AX.X))
                chain(nc.vector.tensor_scalar(SKIP[:, :], NTF[:, :], -float(ETILE), float(REGION), ALU.mult, ALU.add))
                chain(nc.vector.tensor_tensor(PAST[:, :, :], spread(iota_tiles[0:1, :], 2, EXPERTS), spread(INC[:, :], 1, ETILES), ALU.is_ge))
                chain(nc.vector.tensor_tensor(PSKIP[:, :, :], PAST[:, :, :], spread(SKIP[:, :], 1, ETILES), ALU.mult))
                chain(nc.vector.reduce_sum(EOF[:, :], PAST[:, :, :], AX.X))
                chain(nc.vector.reduce_sum(ROF[:, :], PSKIP[:, :, :], AX.X))
                chain(nc.vector.scalar_tensor_tensor(out=RO2[:, :], in0=iota_tiles[0:1, :], scalar=float(ETILE), in1=ROF[:, :],
                                                     op0=ALU.mult, op1=ALU.add))
                chain(nc.vector.tensor_copy(META[:, 0, :], RO2[:, :]))
                nc.vector.tensor_scalar(META[:, 1, :], EOF[:, :], float(EXPERTS - 1), None, ALU.min).then_inc(meta_done, 1)

                def body(it, shared, first):
                    dve.wait_ge(tx_ready, it + 1)
                    if not first:
                        dve.wait_ge(h_ready, it * 2)
                    nc.vector.tensor_copy(XTB[:, :, :], TX[:, :].rearrange("p (a c) -> p a c", a=2)).then_inc(tx_out, 1)
                    if shared:
                        if not first:
                            dve.wait_ge(z_ready, it)
                        for c in range(2):
                            dve.wait_ge(sgs_done, it * 2 + c + 1)
                            nc.vector.scalar_tensor_tensor(out=HS[:, c, :], in0=SH[1][:, c * UTOK:(c + 1) * UTOK], scalar=BS[:, 1, c:c + 1],
                                                           in1=SGS[:, c, :], op0=ALU.add, op1=ALU.mult).then_inc(hs_done, 1)
                    if not first:
                        dve.wait_ge(y_ready, it * 2)
                    for p in range(2):
                        dve.wait_ge(sg_done, it * 2 + p + 1)
                        nc.vector.scalar_tensor_tensor(out=HT[:, p, :], in0=H[p][:, ETILE:2 * ETILE], scalar=WB[:, p, 385:386],
                                                       in1=SG[:, p, :], op0=ALU.add, op1=ALU.mult).then_inc(ht_done, 1)
                    if shared:
                        dve.wait_ge(z_ready, it + 1)
                        if not first:
                            dve.wait_ge(x_done, it)
                        nc.vector.tensor_tensor(ZB[:, :, :], ZP[:, 0:UT * DIM].rearrange("p (t d) -> p t d", t=UT),
                                                spread(BS2[:, :], 1, UT), ALU.add).then_inc(zb_done, 1)
                        dve.wait_ge(zb_done, it + 1)
                        here = X[:, bass.ds(it * UT, UT), :]
                        nc.vector.scalar_tensor_tensor(out=here, in0=ZB[:, :, :], scalar=TG[:, 1:2], in1=here, op0=ALU.mult,
                                                       op1=ALU.add).then_inc(x_done, 1)
                    for p in range(2):
                        dve.wait_ge(y_ready, it * 2 + p + 1)
                        if not first:
                            dve.wait_ge(yw_done, it * 4)
                        nc.vector.tensor_tensor(YB[:, p, :, :], (YP if p == 0 else PS[7])[:, 0:2 * DIM].rearrange("p (a d) -> p a d", a=2),
                                                spread(B2B[:, p, :], 1, 2), ALU.add).then_inc(yb_done, 1)

                run_b(dve, body)

            @block.gpsimd
            def _(pool):
                def body(it, shared, first):
                    for p in range(2):
                        for a in range(2):
                            wait_apart(pool, (yw_done, it * 4 + p * 2 + a + 1))
                            nc.gpsimd.indirect_dma_start(
                                results[:, :], bass.IndirectOffsetOnAxis(ap=XB[:, p, a, DIM + 1:DIM + 2].bitcast(i32), axis=0),
                                YW[:, p, a, :], None).then_inc(sent[p], 16)

                run_b(pool, body)
                pool.wait_ge(sent[0], 32 * BODIES)
                pool.wait_ge(sent[1], 32 * BODIES)

        with ExitStack() as own:
            NB = 4
            YC = own.enter_context(nc.sbuf_tensor("YC", [128, NB, TOPK, CG, DIM], f32))
            YSUM = own.enter_context(nc.sbuf_tensor("YSUM", [128, NB, CG, DIM], f32))
            y_in = [sem(f"y_in{b}") for b in range(NB)]
            ysum_done, out_ready, stored = sem("ysum_done"), sem("out_ready"), sem("stored")
            block = own.enter_context(nc.Block())
            y_tiles = results[0:TOPK * TOKENS, :].rearrange("(s a p) d -> s p a d", s=TOPK, p=128)
            CSTEPS = TILES // CG

            def run_c(engine, body):
                for b in range(NB):
                    body(0, b, True)
                with engine.Fori(1, CSTEPS // NB) as it:
                    for b in range(NB):
                        body(it, b, False)

            @block.sync
            def _(sp):
                def body(it, b, first):
                    n = it * NB + b
                    if not first:
                        sp.wait_ge(ysum_done, n - NB + 1)
                    for s in range(TOPK):
                        sp.dma_start(YC[:, b, s, :, :], y_tiles[s, :, bass.ds(n * CG, CG), :]).then_inc(y_in[b], 16)

                run_c(sp, body)

            @block.vector
            def _(dve):
                def body(it, b, first):
                    n = it * NB + b
                    dve.wait_ge(y_in[b], 32 * (it + 1))
                    if not first:
                        dve.wait_ge(out_ready, n - NB + 1)
                    nc.vector.tensor_tensor(YSUM[:, b, :, :], YC[:, b, 0, :, :], YC[:, b, 1, :, :], ALU.add).then_inc(ysum_done, 1)
                    dve.wait_ge(ysum_done, n + 1)
                    here = X[:, bass.ds(n * CG, CG), :]
                    nc.vector.tensor_tensor(here, here, YSUM[:, b, :, :], ALU.add).then_inc(out_ready, 1)

                run_c(dve, body)

            @block.scalar
            def _(act):
                def body(it, b, first):
                    n = it * NB + b
                    act.wait_ge(out_ready, n + 1)
                    act.dma_start(out_tiles[:, bass.ds(n * CG, CG), :], X[:, bass.ds(n * CG, CG), :]).then_inc(stored, 16)

                run_c(act, body)
                act.wait_ge(stored, 16 * CSTEPS)


DVE_LINKS, POOL_LINKS = 27, 10

CONST_WIDTHS = (("ident", 128), ("hmask", HG), ("iota8", EXPERTS), ("base8", EXPERTS), ("tri8", EXPERTS * EXPERTS),
                ("iota_tiles", ETILES), ("i2", 128), ("tri", 128), ("rank", 128), ("ones", 128))


def shape_constants(np):
    p = np.arange(128)
    q, seq = p % SEQ, p // SEQ
    tables = {
        "ident": np.eye(128),
        "hmask": (p[:, None] // DK) % HG == np.arange(HG)[None, :],
        "iota8": np.tile(np.arange(EXPERTS), (128, 1)),
        "base8": np.tile(np.arange(EXPERTS) * REGION, (128, 1)),
        "tri8": np.tile((np.arange(EXPERTS)[None, :] <= np.arange(EXPERTS)[:, None]).reshape(1, -1), (128, 1)),
        "iota_tiles": np.tile(np.arange(ETILES), (128, 1)),
        "i2": q[:, None] == q[None, :],
        "tri": np.where((seq[:, None] == seq[None, :]) & (q[None, :] > q[:, None]), NEG, 0.0),
        "rank": p[:, None] < p[None, :],
        "ones": np.ones((128, 128)),
    }
    consts = np.concatenate([tables[n].astype(np.float32) for n, _ in CONST_WIDTHS], axis=1)
    dest = np.arange(TOPK)[None, :, None] * TOKENS + np.arange(TILES)[None, None, :] * TILE + p[:, None, None]
    pad = np.zeros((PADS * ETILE, ROW), np.float32)
    pad.view(np.int32)[:, DIM + 1] = TOPK * TOKENS + np.arange(PADS * ETILE)
    return consts, dest.astype(np.int32), pad


def kernel(**inputs):
    import numpy as np
    import concourse.bacc as bacc
    from concourse.bass_utils import run_bass_kernel_spmd

    def w(name):
        return np.asarray(inputs["L0_ffn_" + name])

    consts, dest, pad = shape_constants(np)
    experts = np.concatenate([w("w1").transpose(0, 2, 1), w("w3").transpose(0, 2, 1), w("w2").transpose(0, 2, 1),
                              w("b1")[:, :, None], w("b3")[:, :, None]], axis=2).reshape(EXPERTS * 128, WROW)
    arrays = {
        "x": inputs["x"], "ctx_in": inputs["ctx_1024"], "mask": inputs["mask_BxS2_ik0"], "g_xattn": inputs["g_xattn"],
        "g_ffn": inputs["g_ffn"], "wq": inputs["L0_xattn_WQ"], "wk": inputs["L0_xattn_WK"], "wv": inputs["L0_xattn_WV"],
        "wo": inputs["L0_xattn_WO"], "gate_w": w("gate_w").T, "gate_b": w("gate_b"), "experts": experts, "b2": w("b2"),
        "ws1": w("ws1").T, "bs1": w("bs1").reshape(SHARED // 128, 128).T, "ws3": w("ws3").T,
        "bs3": w("bs3").reshape(SHARED // 128, 128).T, "ws2": w("ws2").T, "bs2": w("bs2"),
        "consts": consts, "dest_rows": dest, "pad_rows": pad,
    }
    nc = bacc.Bacc("TRN2", target_bir_lowering=False, num_devices=1)
    feed, args = {}, {}
    for name, a in arrays.items():
        a = np.ascontiguousarray(np.asarray(a))
        feed["in_" + name] = a
        args[name] = nc.dram_tensor("in_" + name, a.shape, mybir.dt.from_np(a.dtype), kind="ExternalInput").ap()
    args["out"] = nc.dram_tensor("out", (BATCH, SEQ, DIM), mybir.dt.float32, kind="ExternalOutput").ap()
    build_program(nc, **args)
    r = run_bass_kernel_spmd(nc, [feed], core_ids=[0])
    return r.results[0]["out"]
```

```python
import concourse.bass as bass
from concourse import mybir
from contextlib import ExitStack

BATCH, SEQ, DIM, HEADS = 128, 64, 128, 16
DK = DIM // HEADS
EXPERTS, INTER, TOPK, SHARED = 8, 128, 2, 256
TOKENS = BATCH * SEQ
TILE = 128
TILES = TOKENS // TILE
UT = 2
UNITS = TILES // UT
UTOK = UT * TILE
GT = 2 * UT
GROUPS = TILES // GT
NEG = -1.0e9
EPS = 1e-5
SCORE_SCALE = float(DK) ** -0.5
HG = 4
VW = 2 * DK + 2

ROW = DIM + 2
ETILE = 256
REGION = TOKENS + ETILE
SPARE = EXPERTS * REGION
ETILES = (TOPK * TOKENS // ETILE + EXPERTS - 1 + 1) // 2 * 2
SPARES = ETILES - TOPK * TOKENS // ETILE
PADS = EXPERTS + SPARES
WROW = 3 * INTER + 2 + DIM
SLOTS = 8
CG = 4


class At:

    def __init__(self, it, k):
        self.n = it * 2 + k
        self.half = it + k // 2
        self.par = k % 2
        self.known = isinstance(it, int)

    def exists(self):
        return (not self.known) or 0 <= self.n < UNITS

    def later_than(self, m):
        return (not self.known) or self.n >= m


class Links:

    def __init__(self, engine, sem):
        self.engine, self.sem, self.count, self.base = engine, sem, 0, 0

    def done(self, ins):
        ins.then_inc(self.sem, 1)
        self.count += 1

    def wait(self, apart=False):
        if apart:
            wait_apart(self.engine, (self.sem, self.base + self.count))
        else:
            self.engine.wait_ge(self.sem, self.base + self.count)


def wait_apart(engine, *waits):
    for s, v in waits:
        engine.wait_ge(s, v)
    engine.nop(nofuse=True)


def spread(ap, axis, n):
    wide = ap.unsqueeze(axis)
    shape = list(wide.shape)
    shape[axis] = n
    return wide.broadcast_to(shape)


def build_program(nc, x, ctx_in, mask, g_xattn, g_ffn, wq, wk, wv, wo, gate_w, gate_b, experts,
                  ws1, bs1, ws3, bs3, ws2, bs2, consts, dest_rows, pad_rows, out):
    f32, bf16, i32, u32 = mybir.dt.float32, mybir.dt.bfloat16, mybir.dt.int32, mybir.dt.uint32
    ALU, ACT, AX = mybir.AluOpType, mybir.ActivationFunctionType, mybir.AxisListType

    x_tiles = x.rearrange("(a r) s d -> (r s) a d", r=2)
    ctx_tiles = ctx_in.rearrange("(a r) s d -> (r s) a d", r=2)
    out_tiles = out.rearrange("(a r) s d -> (r s) a d", r=2)
    mask_rows = mask.rearrange("(a r) s -> a (r s)", r=2)

    routed = nc.dram_tensor("routed_rows", [SPARE + SPARES * ETILE, ROW], f32, kind="Internal").ap()
    results = nc.dram_tensor("expert_results", [TOPK * TOKENS + PADS * ETILE, DIM], f32, kind="Internal").ap()

    ctx = ExitStack()
    with ctx:
        def sb(name, shape, dt=f32):
            return ctx.enter_context(nc.sbuf_tensor(name, shape, dt))

        def sem(name):
            return ctx.enter_context(nc.semaphore(name))

        X = sb("X", [128, TILES, DIM])
        X2T = sb("X2T", [128, TOKENS])
        CST = sb("CST", [128, consts.shape[1]])
        DEST = sb("DEST", [128, TOPK, TILES], i32)
        at = {}
        pos = 0
        for name, width in CONST_WIDTHS:
            at[name] = CST[:, pos:pos + width]
            pos += width
        ident, hmask, iota8, base8, tri8, iota_tiles = (
            at[n] for n in ("ident", "hmask", "iota8", "base8", "tri8", "iota_tiles"))
        IB = sb("IB", [128, 128], bf16)
        TRI = sb("TRI", [128, SEQ], bf16)
        RANK = sb("RANK", [128, 128], bf16)
        ONES = sb("ONES", [128, 128], bf16)
        TG = sb("TG", [128, 2])
        NM = sb("NM", [128, TILES])
        CARRY = sb("CARRY", [128, GT + 1, EXPERTS], bf16)
        WQ, WK, WV, WO = (sb(n, [128, DIM]) for n in ("WQ", "WK", "WV", "WO"))
        GW = sb("GW", [128, EXPERTS])
        GB = sb("GB", [128, EXPERTS])
        WS1, WS3 = sb("WS1", [128, SHARED]), sb("WS3", [128, SHARED])
        WS2 = sb("WS2", [128, SHARED // 128, DIM])
        BS = sb("BS", [128, 2, SHARED // 128])
        BS2 = sb("BS2", [128, DIM])

        PS = [ctx.enter_context(nc.psum_tensor(f"PS{i}", [128, 512], f32)) for i in range(8)]

        with ExitStack() as own:
            MI = own.enter_context(nc.sbuf_tensor("MI", [TILES, TILE], i32))
            MF = own.enter_context(nc.sbuf_tensor("MF", [TILES, TILE], f32))
            G2 = own.enter_context(nc.sbuf_tensor("G2", [128, 2], f32))
            loaded, mask_float, mask_turned, setup = (sem(n) for n in ("loaded", "mask_float", "mask_turned", "setup"))
            block = own.enter_context(nc.Block())
            loads = [(CST[:, :], consts), (DEST[:, :, :], dest_rows), (MI[:, :], mask_rows),
                     (G2[:, 0:1], g_xattn.partition_broadcast(128)), (G2[:, 1:2], g_ffn.partition_broadcast(128)),
                     (WQ[:, :], wq), (WK[:, :], wk), (WV[:, :], wv), (WO[:, :], wo), (GW[:, :], gate_w),
                     (GB[:, :], gate_b.partition_broadcast(128)), (WS1[:, :], ws1), (WS3[:, :], ws3),
                     (WS2[:, :, :], ws2.rearrange("(c p) d -> p c d", p=128)),
                     (BS[:, 0, :], bs1), (BS[:, 1, :], bs3),
                     (BS2[:, :], bs2.partition_broadcast(128))]
            HALF_L = len(loads) // 2

            @block.sync
            def _(sp):
                for dst, src in loads[:HALF_L]:
                    sp.dma_start(dst, src).then_inc(loaded, 16)

            @block.scalar
            def _(act):
                for dst, src in loads[HALF_L:]:
                    act.dma_start(dst, src).then_inc(loaded, 16)
                act.wait_ge(loaded, 16 * len(loads))
                nc.scalar.activation(TG[:, :], G2[:, :], ACT.Tanh).then_inc(setup, 1)

            @block.vector
            def _(dve):
                dve.wait_ge(loaded, 16 * len(loads))
                nc.vector.tensor_scalar(MF[:, :], MI[:, :], 0.0, None, ALU.is_equal).then_inc(mask_float, 1)
                for dst, name in ((IB, "ident"), (TRI, "tri"), (RANK, "rank"), (ONES, "ones")):
                    nc.vector.tensor_copy(dst[:, :], at[name]).then_inc(setup, 1)
                nc.vector.memset(CARRY[:, :, :], 0.0).then_inc(setup, 1)
                dve.wait_ge(mask_turned, 1)
                nc.vector.tensor_copy(NM[:, :], PS[0][:, 0:TILES]).then_inc(setup, 1)

            @block.tensor
            def _(pe):
                pe.wait_ge(loaded, 16 * len(loads))
                pe.wait_ge(mask_float, 1)
                nc.tensor.transpose(PS[0][:, 0:TILES], MF[:, :], ident[0:TILES, 0:TILES]).then_inc(mask_turned, 1)

            @block.gpsimd
            def _(pool):
                pool.wait_ge(setup, 7)

        with ExitStack() as own:
            def sa(name, shape, dt=f32):
                return own.enter_context(nc.sbuf_tensor(name, shape, dt))

            C = sa("C", [128, 2, UT, DIM])
            XN = sa("XN", [128, 2, UT, DIM])
            ST1, ST2 = sa("ST1", [128, UT, 6]), sa("ST2", [128, UT, 6])
            MV1, MV2 = sa("MV1", [128, UT, 2]), sa("MV2", [128, UT, 2])
            RS1, RS2, VE1, VE2 = (sa(n, [128, UT]) for n in ("RS1", "RS2", "VE1", "VE2"))
            RM1 = sa("RM1", [128, UT])
            HALFNEG, EPSV = sa("HALFNEG", [128, UT]), sa("EPSV", [128, UT])
            XCT = sa("XCT", [128, 2, UTOK])
            QT = sa("QT", [128, 2 * UT, SEQ])
            KB = sa("KB", [128, 2 * UT, HG, SEQ])
            MP = sa("MP", [128, 2, UT, SEQ], bf16)
            MX = sa("MX", [128, HG, 8])
            P = sa("P", [128, 2, HG, 512])
            PT = sa("PT", [128, 2, 512])
            VX = sa("VX", [128, 2, 2, UT, HEADS // 2, VW])
            R = sa("R", [128, UT * 8, 2])
            A = sa("A", [128, UT, DIM])
            AT = sa("AT", [128, UTOK])
            X2 = sa("X2", [128, GT, DIM])
            X2G = sa("X2G", [128, GT * TILE])
            LG = sa("LG", [128, GT, EXPERTS])
            M8 = sa("M8", [128, GT, 8])
            I8 = sa("I8", [128, GT, 8], u32)
            IF = sa("IF", [128, GT, TOPK])
            OH = sa("OH", [128, GT, TOPK, EXPERTS])
            OHS = sa("OHS", [128, GT, EXPERTS], bf16)
            NL = sa("NL", [128, GT, EXPERTS + TOPK])
            EX = sa("EX", [128, GT, EXPERTS + TOPK])
            Z, RZ = sa("Z", [128, GT]), sa("RZ", [128, GT])
            RB = sa("RB", [128, GT, EXPERTS])
            OP = sa("OP", [128, GT, TOPK, EXPERTS])
            PF = sa("PF", [128, GT, TOPK])
            IDX = sa("IDX", [128, TOPK, GT], i32)
            STAGE = sa("STAGE", [128, TOPK, GT, ROW])

            S, T, M0, M1 = PS[0:4], PS[4:6], PS[6], PS[7]

            x_in = [sem("x_in0"), sem("x_in1")]
            c_in = [sem("c_in0"), sem("c_in1")]
            (consts_a, stat1, xn_done, mp_done, xc_ready, xc_out, qk_ready, q_out, k_out, v_ready, v_out, s_ready,
             sub_done, exp_done, t_ready, pt_out, pv_ready, norm_done, at_ready, at_out,
             wo_ready, resid, stat2, rs2_done, xn2_done, x2t_ready, x2t_out, x2t_saved, logits_ready, logits_used,
             nl_done, e_done, w_done, oh_done, rank_ready, rank_used, idx_done, stage_x, stage_dest, scattered,
             dve_own, pool_own) = (sem(n) for n in (
                 "consts_a", "stat1", "xn_done", "mp_done", "xc_ready", "xc_out", "qk_ready", "q_out", "k_out",
                 "v_ready", "v_out", "s_ready", "sub_done", "exp_done", "t_ready", "pt_out", "pv_ready", "norm_done", "at_ready", "at_out", "wo_ready", "resid", "stat2", "rs2_done",
                 "xn2_done", "x2t_ready", "x2t_out", "x2t_saved", "logits_ready", "logits_used", "nl_done", "e_done",
                 "w_done", "oh_done", "rank_ready", "rank_used", "idx_done", "stage_x", "stage_dest", "scattered",
                 "dve_own", "pool_own"))

            block = own.enter_context(nc.Block())

            def around(it, k):
                return tuple(At(it, k + d) for d in (2, 1, 0, -1, -2, -3, -4))

            TRIPS = (UNITS - 6) // 2
            BEFORE = [(0, k) for k in range(-2, 6)]
            AFTER = [(TRIPS, k) for k in range(2, 10)]

            def run(engine, step, links=None, per_trip=0):
                for it, k in BEFORE:
                    step(it, k)
                first = links.count if links else 0
                with engine.Fori(2, TRIPS) as it:
                    if links:
                        links.base, links.count = first + (it - 2) * per_trip, 0
                    step(it, 2)
                    step(it, 3)
                    if links:
                        assert links.count == per_trip, (links.count, per_trip)
                if links:
                    links.base, links.count = 0, first + (TRIPS - 2) * per_trip
                for it, k in AFTER:
                    step(it, k)

            def tiles_of(u):
                return bass.ds(u.n * UT, UT)

            @block.sync
            def _(sp):
                def load_x(u):
                    sp.dma_start(X[:, tiles_of(u), :], x_tiles[:, tiles_of(u), :]).then_inc(x_in[u.par], 16)

                def load_c(u):
                    sp.dma_start(C[:, u.par, :, :], ctx_tiles[:, tiles_of(u), :]).then_inc(c_in[u.par], 16)

                load_x(At(0, 0))
                load_c(At(0, 0))
                load_x(At(0, 1))
                load_c(At(0, 1))

                def step(it, k):
                    e, f, i, u, w, v, y = around(it, k)
                    f2 = At(it, k + 3)
                    if f2.exists() and f2.later_than(2):
                        sp.wait_ge(x_in[f.par], 16 * (f.half + 1))
                        load_x(f2)
                    if f2.exists() and f2.later_than(2):
                        sp.wait_ge(xc_ready, f.n + 1)
                        load_c(f2)
                    if v.exists() and v.par:
                        sp.wait_ge(x2t_out, v.n + 1)
                        sp.dma_start(X2T[:, bass.ds(v.half * (GT * TILE), GT * TILE)], X2G[:, :]).then_inc(x2t_saved, 16)

                run(sp, step)
                sp.wait_ge(x2t_saved, 16 * GROUPS)

            @block.tensor
            def _(pe):
                pe.wait_ge(consts_a, 3)

                def scores(i, pair):
                    for g in pair:
                        nc.tensor.matmul(S[g][:, :], IB[:, :], spread(MP[:, i.par, :, :], 2, HG), start=True, stop=False,
                                         skip_group_check=True)
                    for t in range(UT):
                        for g in pair:
                            for b in range(2):
                                rows = slice(32 * g, 32 * g + 32)
                                last = nc.tensor.matmul(
                                    S[g][SEQ * b:SEQ * b + SEQ, t * HG * SEQ:(t + 1) * HG * SEQ], QT[rows, 2 * t + b, :],
                                    KB[rows, 2 * t + b, :, :], start=False, stop=(t == 1), tile_position=(32 * g, SEQ * b),
                                    skip_group_check=True)
                    last.then_inc(s_ready, 1)

                def turn_p(u, g):
                    if u.later_than(1) or g >= 2:
                        pe.wait_ge(pt_out, u.n * 4 + g - 1)
                    for c in range(4):
                        last = nc.tensor.transpose(T[g % 2][:, 128 * c:128 * c + 128],
                                                   P[:, u.par, g, 128 * c:128 * c + 128], ident)
                    last.then_inc(t_ready, 1)

                def p_v(u, g):
                    pe.wait_ge(pt_out, u.n * 4 + g + 1)
                    for t in range(UT):
                        for jp in range(2):
                            o = (t * 8 + g * 2 + jp) * VW
                            for b in range(2):
                                c = (2 * t + jp) * 128 + SEQ * b
                                last = nc.tensor.matmul(M0[SEQ * b:SEQ * b + SEQ, o:o + VW], PT[:, g % 2, c:c + SEQ],
                                                        VX[:, u.par, b, t, 2 * g + jp, :], start=True, stop=True,
                                                        tile_position=(0, SEQ * b))
                    return last

                def m0_free(v, y, w):
                    if v.exists() and v.par:
                        pe.wait_ge(logits_used, v.half + 1)
                    if y.exists() and y.par:
                        pe.wait_ge(rank_used, y.half + 1)

                def step(it, k):
                    e, f, i, u, w, v, y = around(it, k)
                    if i.exists():
                        pe.wait_ge(q_out, i.n + 1)
                        pe.wait_ge(k_out, i.n + 1)
                        pe.wait_ge(mp_done, i.n + 1)
                        if i.later_than(1):
                            pe.wait_ge(sub_done, i.n * HG - 2)
                        scores(i, (0, 1))
                    if w.exists():
                        pe.wait_ge(norm_done, w.n + 1)
                        for t in range(UT):
                            last = nc.tensor.transpose(T[0][:, t * TILE:(t + 1) * TILE], A[:, t, :], ident)
                        last.then_inc(at_ready, 1)
                    if v.exists():
                        pe.wait_ge(xn2_done, v.n + 1)
                        if not w.exists():
                            pe.wait_ge(x2t_out, v.n)
                        for t in range(UT):
                            last = nc.tensor.transpose(T[0][:, UTOK + t * TILE:UTOK + (t + 1) * TILE], X2[:, v.par * UT + t, :], ident)
                        last.then_inc(x2t_ready, 1)
                    if i.exists():
                        if i.later_than(1):
                            pe.wait_ge(sub_done, i.n * HG)
                        scores(i, (2, 3))
                    if y.exists() and y.par:
                        pe.wait_ge(oh_done, y.half + 1)
                        nc.tensor.matmul(M0[:, 0:GT * EXPERTS], RANK[:, :], OHS[:, :, :], start=True, stop=False)
                        nc.tensor.matmul(M0[:, 0:GT * EXPERTS], ONES[:, :], CARRY[:, 0:GT, :], start=False,
                                         stop=True).then_inc(rank_ready, 1)
                    if v.exists() and v.par:
                        pe.wait_ge(x2t_out, v.n + 1)
                        for t in range(GT):
                            last = nc.tensor.matmul(M0[:, t * EXPERTS:(t + 1) * EXPERTS], X2G[:, t * TILE:(t + 1) * TILE],
                                                    GW[:, :], start=True, stop=True)
                        last.then_inc(logits_ready, 1)
                    if w.exists():
                        pe.wait_ge(at_out, w.n + 1)
                        if i.exists():
                            pe.wait_ge(v_out, 4 * (i.n + 1))
                        for t in range(UT):
                            last = nc.tensor.matmul(M1[:, t * DIM:(t + 1) * DIM], AT[:, t * TILE:(t + 1) * TILE], WO[:, :],
                                                    start=True, stop=True)
                        last.then_inc(wo_ready, 1)
                    if u.exists():
                        if v.exists():
                            pe.wait_ge(x2t_out, v.n + 1)
                        if w.exists():
                            pe.wait_ge(at_out, w.n + 1)
                        pe.wait_ge(exp_done, u.n * 2 + 1)
                        turn_p(u, 0)
                        turn_p(u, 1)
                    if f.exists():
                        pe.wait_ge(xn_done, f.n + 1)
                        pe.wait_ge(c_in[f.par], 16 * (f.half + 1))
                        m0_free(v, y, w)
                        for t in range(UT):
                            nc.tensor.transpose(M0[:, t * TILE:(t + 1) * TILE], XN[:, f.par, t, :], ident)
                        for t in range(UT):
                            last = nc.tensor.transpose(M0[:, UTOK + t * TILE:UTOK + (t + 1) * TILE], C[:, f.par, t, :], ident)
                        last.then_inc(xc_ready, 1)
                    if u.exists():
                        pe.wait_ge(exp_done, u.n * 2 + 2)
                        if f.exists():
                            pe.wait_ge(xc_out, f.n + 1)
                        else:
                            m0_free(v, y, w)
                        p_v(u, 0)
                        turn_p(u, 2)
                    if f.exists():
                        pe.wait_ge(xc_out, f.n + 1)
                        if w.exists():
                            pe.wait_ge(resid, w.n + 1)
                        elif f.later_than(1):
                            pe.wait_ge(v_out, 4 * f.n)
                        nc.tensor.matmul(M1[:, 0:UTOK], WQ[:, :], XCT[:, 0, :], start=True, stop=True)
                        nc.tensor.matmul(M1[:, UTOK:2 * UTOK], WK[:, :], XCT[:, 1, :], start=True, stop=True).then_inc(qk_ready, 1)
                    if u.exists():
                        p_v(u, 1)
                        turn_p(u, 3)
                        p_v(u, 2)
                        p_v(u, 3).then_inc(pv_ready, 1)
                    if f.exists():
                        pe.wait_ge(q_out, f.n + 1)
                        pe.wait_ge(k_out, f.n + 1)
                        for t in range(UT):
                            last = nc.tensor.matmul(M1[:, t * DIM:(t + 1) * DIM], XCT[:, 1, t * TILE:(t + 1) * TILE], WV[:, :],
                                                    start=True, stop=True)
                        last.then_inc(v_ready, 1)

                run(pe, step)

            @block.scalar
            def _(act):
                def copy(dst, src):
                    return nc.scalar.activation(dst, src, ACT.Copy)

                def p_out(u, g):
                    act.wait_ge(t_ready, u.n * 4 + g + 1)
                    copy(PT[:, g % 2, :], T[g % 2][:, :]).then_inc(pt_out, 1)

                def step(it, k):
                    e, f, i, u, w, v, y = around(it, k)
                    if y.exists() and y.par:
                        act.wait_ge(nl_done, y.half + 1)
                        nc.scalar.activation(EX[:, :, :], NL[:, :, :], ACT.Exp).then_inc(e_done, 1)
                    if w.exists():
                        act.wait_ge(at_ready, w.n + 1)
                        if v.exists():
                            act.wait_ge(x2t_ready, v.n + 1)
                        copy(AT[:, :], T[0][:, 0:UTOK]).then_inc(at_out, 1)
                    if v.exists():
                        act.wait_ge(x2t_ready, v.n + 1)
                        if not v.par and v.later_than(2):
                            act.wait_ge(x2t_saved, 16 * v.half)
                        copy(X2G[:, v.par * UTOK:(v.par + 1) * UTOK], T[0][:, UTOK:2 * UTOK]).then_inc(x2t_out, 1)
                    if u.exists():
                        p_out(u, 0)
                        p_out(u, 1)
                    if f.exists():
                        act.wait_ge(xc_ready, f.n + 1)
                        copy(XCT[:, :, :], M0[:, :]).then_inc(xc_out, 1)
                    if u.exists():
                        p_out(u, 2)
                    if f.exists():
                        act.wait_ge(qk_ready, f.n + 1)
                        copy(QT[:, :, :], M1[:, 0:UTOK]).then_inc(q_out, 1)
                    if u.exists():
                        p_out(u, 3)
                    def soften(c):
                        act.wait_ge(sub_done, i.n * HG + 2 * c + 2)
                        nc.scalar.activation(P[:, i.par, 2 * c:2 * c + 2, :], P[:, i.par, 2 * c:2 * c + 2, :], ACT.Exp,
                                             scale=SCORE_SCALE).then_inc(exp_done, 1)
                    if i.exists():
                        soften(0)
                    if f.exists():
                        act.wait_ge(v_ready, f.n + 1)
                        for b in range(2):
                            for j in range(2):
                                copy(VX[SEQ * j:SEQ * j + SEQ, f.par, b, :, :, DK * j:DK * j + DK],
                                     M1[SEQ * b:SEQ * b + SEQ, 0:UT * DIM].rearrange("p (t h c) -> p t h c", t=UT, c=16)
                                     [:, :, :, DK * j:DK * j + DK]).then_inc(v_out, 1)
                    if v.exists() and v.par:
                        act.wait_ge(xn2_done, v.n + 1)
                        if v.later_than(2):
                            act.wait_ge(scattered, 16 * TOPK * GT * v.half)
                        copy(STAGE[:, :, :, 0:DIM], spread(X2[:, :, :], 1, TOPK)).then_inc(stage_x, 1)
                    if i.exists():
                        soften(1)

                run(act, step)

            @block.vector
            def _(dve):
                own_v = Links(dve, dve_own)
                for p in range(2):
                    own_v.done(nc.vector.memset(VX[:, p, :, :, :, :].rearrange("p b t h c -> p (b t h c)"), 0.0))
                own_v.wait()
                for j in range(2):
                    for p in range(2):
                        ins = nc.vector.memset(VX[SEQ * j:SEQ * j + SEQ, p, :, :, :, 2 * DK + j:2 * DK + j + 1].rearrange("p b t h c -> p (b t h) c"), 1.0)
                        if p == 1:
                            ins.then_inc(consts_a, 1)
                        else:
                            own_v.done(ins)
                own_v.wait()
                nc.vector.memset(EPSV[:, :], EPS)
                nc.vector.memset(HALFNEG[:, :], -0.5).then_inc(consts_a, 1)

                def statistics(rows, st, mv, done):
                    for t in range(UT):
                        last = nc.vector.bn_stats(st[:, t, :], rows[t])
                    own_v.done(last)
                    own_v.wait(apart=True)
                    for t in range(UT):
                        last = nc.vector.bn_aggr(mv[:, t, :], st[:, t, :])
                    last.then_inc(done, 1)

                def choose(w):
                    g1 = w.half + 1
                    dve.wait_ge(logits_ready, g1)
                    nc.vector.tensor_tensor(LG[:, :, :], M0[:, 0:GT * EXPERTS].rearrange("p (t e) -> p t e", t=GT),
                                            spread(GB[:, :], 1, GT), ALU.add).then_inc(logits_used, 1)
                    wait_apart(dve, (logits_used, g1))
                    for t in range(GT):
                        ins = nc.vector.max(M8[:, t, :], LG[:, t, :])
                    own_v.done(ins)
                    own_v.wait()
                    nc.vector.tensor_tensor(NL[:, :, 0:EXPERTS], LG[:, :, :], M8[:, :, 0:1].broadcast_to([128, GT, EXPERTS]),
                                            ALU.subtract)
                    nc.vector.tensor_tensor(NL[:, :, EXPERTS:], M8[:, :, 0:TOPK], M8[:, :, 0:1].broadcast_to([128, GT, TOPK]),
                                            ALU.subtract).then_inc(nl_done, 1)
                    for t in range(GT):
                        ins = nc.vector.max_index(I8[:, t, :], M8[:, t, :], LG[:, t, :])
                    own_v.done(ins)
                    own_v.wait()
                    own_v.done(nc.vector.tensor_copy(IF[:, :, :], I8[:, :, 0:TOPK]))
                    own_v.wait()
                    own_v.done(nc.vector.tensor_tensor(OH[:, :, :, :], spread(spread(iota8, 1, TOPK), 1, GT),
                                                       spread(IF[:, :, :], 3, EXPERTS), ALU.is_equal))
                    own_v.wait()
                    own_v.done(nc.vector.tensor_tensor(OHS[:, :, :], OH[:, :, 0, :], OH[:, :, 1, :], ALU.add))
                    own_v.wait()
                    for t in range(GT):
                        ins = nc.vector.tensor_tensor(CARRY[:, t + 1, :], CARRY[:, t, :], OHS[:, t, :], ALU.add)
                        if t < GT - 1:
                            own_v.done(ins)
                            own_v.wait()
                    ins.then_inc(oh_done, 1)

                def place(w):
                    g1 = w.half + 1
                    dve.wait_ge(e_done, g1)
                    own_v.done(nc.vector.reduce_sum(Z[:, :], EX[:, :, 0:EXPERTS], AX.X))
                    own_v.wait()
                    own_v.done(nc.vector.reciprocal(RZ[:, :], Z[:, :]))
                    own_v.wait()
                    if w.later_than(2):
                        dve.wait_ge(scattered, 16 * TOPK * GT * w.half)
                    nc.vector.scalar_tensor_tensor(
                        out=STAGE[:, :, :, DIM].rearrange("p s t -> p t s"), in0=EX[:, :, EXPERTS:], scalar=TG[:, 1:2],
                        in1=spread(RZ[:, :], 2, TOPK), op0=ALU.mult, op1=ALU.mult).then_inc(w_done, 1)
                    dve.wait_ge(rank_ready, g1)
                    nc.vector.tensor_tensor(RB[:, :, :], M0[:, 0:GT * EXPERTS].rearrange("p (t e) -> p t e", t=GT),
                                            spread(base8, 1, GT), ALU.add).then_inc(rank_used, 1)
                    own_v.done(nc.vector.tensor_copy(CARRY[:, 0, :], CARRY[:, GT, :]))
                    dve.wait_ge(rank_used, g1)
                    own_v.done(nc.vector.tensor_tensor(OP[:, :, :, :], OH[:, :, :, :], spread(RB[:, :, :], 2, TOPK), ALU.mult))
                    own_v.wait()
                    own_v.done(nc.vector.reduce_sum(PF[:, :, :], OP[:, :, :, :], AX.X))
                    own_v.wait()
                    nc.vector.tensor_copy(IDX[:, :, :].rearrange("p s t -> p t s"), PF[:, :, :]).then_inc(idx_done, 1)

                def softmax_shift(i, g):
                    bank = S[g][:, :].rearrange("p (c k) -> p c k", c=8)
                    own_v.done(nc.vector.tensor_reduce(out=MX[:, g, :], in_=bank, axis=AX.X, op=ALU.max))
                    own_v.wait()
                    nc.vector.tensor_tensor(P[:, i.par, g, :].rearrange("p (c k) -> p c k", c=8), bank,
                                            spread(MX[:, g, :], 2, SEQ), ALU.subtract).then_inc(sub_done, 1)

                def step(it, k):
                    e, f, i, u, w, v, y = around(it, k)
                    if i.exists():
                        dve.wait_ge(s_ready, 2 * i.n + 1)
                        softmax_shift(i, 0)
                        softmax_shift(i, 1)
                    if v.exists() and v.par:
                        choose(v)
                    if y.exists() and y.par:
                        place(y)
                    if w.exists():
                        dve.wait_ge(wo_ready, w.n + 1)
                        here = X[:, tiles_of(w), :]
                        nc.vector.scalar_tensor_tensor(
                            out=here, in0=M1[:, 0:UT * DIM].rearrange("p (t d) -> p t d", t=UT), scalar=TG[:, 0:1], in1=here,
                            op0=ALU.mult, op1=ALU.add).then_inc(resid, 1)
                        wait_apart(dve, (resid, w.n + 1))
                        statistics([X[:, bass.ds(w.n * UT + t, 1), :] for t in range(UT)], ST2, MV2, stat2)
                    if e.exists():
                        wait_apart(dve, (x_in[e.par], 16 * (e.half + 1)), *[(xn_done, e.n)] * e.later_than(1))
                        statistics([X[:, bass.ds(e.n * UT + t, 1), :] for t in range(UT)], ST1, MV1, stat1)
                    if f.exists():
                        dve.wait_ge(q_out, f.n + 1)
                        kt = M1[:, UTOK:2 * UTOK].rearrange("p (s q) -> p s q", q=SEQ)
                        nc.vector.tensor_tensor(KB[:, :, :, :], spread(kt, 2, HG), spread(spread(hmask, 1, 2 * UT), 3, SEQ),
                                                ALU.mult).then_inc(k_out, 1)
                    if i.exists():
                        dve.wait_ge(s_ready, 2 * i.n + 2)
                        softmax_shift(i, 2)
                        softmax_shift(i, 3)
                    if u.exists():
                        dve.wait_ge(pv_ready, u.n + 1)
                        if u.later_than(1):
                            dve.wait_ge(at_ready, u.n)
                        heads = M0[:, 0:UT * 8 * VW].rearrange("p (h c) -> p h c", c=VW)
                        own_v.done(nc.vector.reciprocal(R[:, :, :], heads[:, :, 2 * DK:VW]))
                        own_v.wait()
                        nc.vector.tensor_tensor(
                            A[:, :, :].rearrange("p t (h j c) -> p (t h) j c", j=2, c=DK),
                            heads[:, :, 0:2 * DK].rearrange("p h (j c) -> p h j c", j=2), spread(R[:, :, :], 3, DK),
                            ALU.mult).then_inc(norm_done, 1)
                    if w.exists():
                        dve.wait_ge(rs2_done, w.n + 1)
                        if not w.par and w.later_than(2):
                            dve.wait_ge(stage_x, w.half)
                            dve.wait_ge(x2t_ready, w.n)
                        for t in range(UT):
                            ins = nc.vector.tensor_scalar(
                                X2[:, w.par * UT + t, :], X[:, bass.ds(w.n * UT + t, 1), :], MV2[:, t, 0:1], RS2[:, t:t + 1],
                                ALU.subtract, ALU.mult)
                        ins.then_inc(xn2_done, 1)

                run(dve, step, own_v, DVE_LINKS)

            @block.gpsimd
            def _(pool):
                own_p = Links(pool, pool_own)
                pool.wait_ge(consts_a, 3)

                def rstd(rs, ve, mv):
                    own_p.done(nc.gpsimd.tensor_tensor(ve[:, :], mv[:, :, 1], EPSV[:, :], ALU.add))
                    own_p.wait()
                    return nc.gpsimd.tensor_tensor(rs[:, :], ve[:, :], HALFNEG[:, :], ALU.pow)

                def scatter(y, s):
                    for t in range(GT):
                        nc.gpsimd.indirect_dma_start(
                            routed[:, :], bass.IndirectOffsetOnAxis(ap=IDX[:, s, t:t + 1], axis=0),
                            STAGE[:, s, t, :], None).then_inc(scattered, 16)

                def step(it, k):
                    e, f, i, u, w, v, y = around(it, k)
                    placing = y.exists() and y.par
                    if placing:
                        if y.later_than(2):
                            pool.wait_ge(scattered, 16 * TOPK * GT * y.half)
                        nc.gpsimd.tensor_copy(STAGE[:, :, :, DIM + 1].bitcast(i32), DEST[:, :, bass.ds(y.half * GT, GT)]).then_inc(stage_dest, 1)
                        wait_apart(pool, (stage_dest, y.half + 1), (stage_x, y.half + 1), (w_done, y.half + 1),
                                   (idx_done, y.half + 1))
                        scatter(y, 0)
                    if w.exists():
                        pool.wait_ge(stat2, w.n + 1)
                        rstd(RS2, VE2, MV2).then_inc(rs2_done, 1)
                    if e.exists():
                        pool.wait_ge(stat1, e.n + 1)
                        own_p.done(rstd(RS1, VE1, MV1))
                        own_p.wait(apart=True)
                        own_p.done(nc.gpsimd.tensor_tensor(RM1[:, :], RS1[:, :], NM[:, tiles_of(e)], ALU.mult))
                        xn = XN[:, e.par, :, :]
                        own_p.done(nc.gpsimd.tensor_tensor(xn, X[:, tiles_of(e), :], spread(MV1[:, :, 0], 2, DIM), ALU.subtract))
                        own_p.wait()
                        nc.gpsimd.tensor_tensor(xn, xn, spread(RM1[:, :], 2, DIM), ALU.mult).then_inc(xn_done, 1)
                    if f.exists():
                        wait_apart(pool, *[(s_ready, 2 * f.n - 2)] * f.later_than(2))
                        nc.gpsimd.tensor_tensor(MP[:, f.par, :, :], spread(TRI[:, :], 1, UT), spread(NM[:, tiles_of(f)], 2, SEQ),
                                                ALU.mult).then_inc(mp_done, 1)
                    if placing:
                        scatter(y, 1)

                run(pool, step, own_p, POOL_LINKS)
                pool.wait_ge(scattered, 16 * TOPK * GT * GROUPS)

        with ExitStack() as own:
            def sa(name, shape, dt=f32):
                return own.enter_context(nc.sbuf_tensor(name, shape, dt))

            CNT, CI, NTI, NTF = sa("CNT", [1, EXPERTS]), sa("CI", [1, EXPERTS], i32), sa("NTI", [1, EXPERTS], i32), sa("NTF", [1, EXPERTS])
            CUM8, INC, SKIP = sa("CUM8", [1, EXPERTS, EXPERTS]), sa("INC", [1, EXPERTS]), sa("SKIP", [1, EXPERTS])
            PAST = sa("PAST", [1, ETILES, EXPERTS])
            PSKIP = sa("PSKIP", [1, ETILES, EXPERTS])
            EOF = sa("EOF", [1, ETILES])
            ROF, RO2 = sa("ROF", [1, ETILES]), sa("RO2", [1, ETILES])
            META = sa("META", [1, ETILES, 2], i32)
            XB = sa("XB", [128, SLOTS, 2, 2, ROW])
            WB = sa("WB", [128, SLOTS, 2, WROW])
            XTB = sa("XTB", [128, 2, 2 * ETILE])
            SG = sa("SG", [128, 2, ETILE])
            HT = sa("HT", [128, 2, 2, ETILE])
            YB = sa("YB", [128, 2, 2, DIM])
            YW = sa("YW", [128, 2, 2, 2, DIM])
            SGS = sa("SGS", [128, 2, UTOK])
            HS = sa("HS", [128, 2, 2, UTOK])
            ZB = sa("ZB", [128, UT, DIM])
            TX, H, SH, ZP, YP = PS[0], PS[1:3], PS[3:5], PS[5], PS[6:8]

            tiles_in = [sem(f"tiles_in{b}") for b in range(SLOTS)]
            sent = [sem(f"sent{b}") for b in range(SLOTS)]
            (count_ready, meta_done, padded, tx_ready, tx_out, h_ready, sg_done, ht_done, y_ready, yb_done, yw_done,
             sh_ready, sgs_done, hs_done, z_ready, zb_done, x_done, meta_own) = (sem(n) for n in (
                 "count_ready", "meta_done", "padded", "tx_ready", "tx_out", "h_ready", "sg_done", "ht_done", "y_ready",
                 "yb_done", "yw_done", "sh_ready", "sgs_done", "hs_done", "z_ready", "zb_done", "x_done", "meta_own"))
            block = own.enter_context(nc.Block())
            STEPS = ETILES // 2

            WITHIN = "the expert's number is capped, and the lists and spare tiles hold every row that follows from the counts"

            def run_b(engine, step):
                for j in range(-1, SLOTS):
                    step(0, j)
                with engine.Fori(1, UNITS // SLOTS) as it:
                    for j in range(SLOTS):
                        step(it, j)
                for j in range(STEPS + 1 - UNITS):
                    step(UNITS // SLOTS, j)

            def is_step(it, j):
                return (not isinstance(it, int)) or 0 <= SLOTS * it + j < STEPS

            def has_shared(it, j):
                return (not isinstance(it, int)) or 0 <= SLOTS * it + j < UNITS

            def later(it, j, m):
                return (not isinstance(it, int)) or SLOTS * it + j >= m

            def slot(j):
                return j % SLOTS, j // SLOTS

            @block.sync
            def _(sp):
                sp.wait_ge(meta_done, 1)
                for e in range(EXPERTS):
                    count = sp.value_load(CI[0:1, e:e + 1], min_val=0, max_val=TOKENS)
                    sp.dma_start(routed[bass.ds(count + e * REGION, ETILE), :], pad_rows[e * ETILE:(e + 1) * ETILE, :]).then_inc(padded, 16)
                sp.dma_start(routed[SPARE:, :], pad_rows[EXPERTS * ETILE:, :]).then_inc(padded, 16)
                sp.wait_ge(padded, 16 * (EXPERTS + 1))

                def step(it, j):
                    if not is_step(it, j):
                        return
                    b, turn = slot(j)
                    if later(it, j, SLOTS):
                        sp.wait_ge(sent[b], 64 * it)
                    _, places = nc.values_load_multi_w_load_instructions(
                        META[0:1, bass.ds((SLOTS * it + j) * 2, 2), :], engines=[mybir.EngineType.SP], min_val=0,
                        max_val=SPARE + (SPARES - 1) * ETILE, skip_runtime_bounds_check_because=WITHIN)
                    for p in range(2):
                        row, expert = places[2 * p], nc.s_assert_within(
                            places[2 * p + 1], 0, EXPERTS - 1, skip_runtime_bounds_check_because=WITHIN)
                        sp.dma_start(XB[:, b, p, :, :], routed[bass.ds(row, ETILE), :].rearrange("(a p) c -> p a c", p=128)).then_inc(tiles_in[b], 16)
                        sp.dma_start(WB[:, b, p, :], experts[bass.ds(expert * 128, 128), :]).then_inc(tiles_in[b], 16)

                run_b(sp, step)

            @block.tensor
            def _(pe):
                nc.tensor.matmul(PS[7][:, 0:EXPERTS], ONES[:, :], CARRY[:, 0, :], start=True, stop=True).then_inc(count_ready, 1)

                def step(it, j):
                    n = SLOTS * it + j
                    if is_step(it, j):
                        pe.wait_ge(tx_out, n + 1)
                        if later(it, j, 1):
                            pe.wait_ge(ht_done, 2 * n)
                        for p in range(2):
                            cols = XTB[:, j % 2, p * ETILE:(p + 1) * ETILE]
                            nc.tensor.matmul(H[p][:, 0:ETILE], WB[:, j % SLOTS, p, 0:128], cols, start=True, stop=True)
                            nc.tensor.matmul(H[p][:, ETILE:2 * ETILE], WB[:, j % SLOTS, p, 128:256], cols, start=True,
                                             stop=True).then_inc(h_ready, 1)
                    if has_shared(it, j):
                        if later(it, j, 1):
                            pe.wait_ge(hs_done, 2 * n)
                        cols = X2T[:, bass.ds(n * UTOK, UTOK)]
                        for c in range(2):
                            nc.tensor.matmul(SH[0][:, c * UTOK:(c + 1) * UTOK], WS1[:, c * 128:c * 128 + 128], cols, start=True, stop=True)
                        for c in range(2):
                            last = nc.tensor.matmul(SH[1][:, c * UTOK:(c + 1) * UTOK], WS3[:, c * 128:c * 128 + 128], cols,
                                                    start=True, stop=True)
                        last.then_inc(sh_ready, 1)
                    if is_step(it, j + 1):
                        b, turn = slot(j + 1)
                        pe.wait_ge(tiles_in[b], 64 * (it + turn + 1))
                        if later(it, j, 0):
                            pe.wait_ge(tx_out, n + 1)
                        for p in range(2):
                            for a in range(2):
                                last = nc.tensor.transpose(TX[:, p * ETILE + a * 128:p * ETILE + a * 128 + 128],
                                                           XB[:, b, p, a, 0:DIM], ident)
                        last.then_inc(tx_ready, 1)
                    if later(it, j, 1):
                        for p in range(2):
                            pe.wait_ge(ht_done, 2 * n - 1 + p)
                            if later(it, j, 2):
                                pe.wait_ge(yb_done, 2 * n - 3 + p)
                            for a in range(2):
                                last = nc.tensor.matmul(YP[p][:, a * DIM:(a + 1) * DIM], HT[:, (j - 1) % 2, p, a * 128:a * 128 + 128],
                                                        WB[:, (j - 1) % SLOTS, p, 256:384], start=True, stop=True)
                            last.then_inc(y_ready, 1)
                        if has_shared(it, j - 1):
                            pe.wait_ge(hs_done, 2 * n)
                            if later(it, j, 2):
                                pe.wait_ge(zb_done, n - 1)
                            for t in range(UT):
                                for c in range(2):
                                    last = nc.tensor.matmul(ZP[:, t * DIM:(t + 1) * DIM], HS[:, (j - 1) % 2, c, t * TILE:(t + 1) * TILE],
                                                            WS2[:, c, :], start=(c == 0), stop=(c == 1))
                            last.then_inc(z_ready, 1)

                run_b(pe, step)

            @block.scalar
            def _(act):
                def step(it, j):
                    n = SLOTS * it + j
                    if is_step(it, j):
                        for p in range(2):
                            act.wait_ge(h_ready, 2 * n + p + 1)
                            nc.scalar.activation(SG[:, p, :], H[p][:, 0:ETILE], ACT.Silu, bias=WB[:, j % SLOTS, p, 384:385]).then_inc(sg_done, 1)
                    if has_shared(it, j):
                        act.wait_ge(sh_ready, n + 1)
                        for c in range(2):
                            nc.scalar.activation(SGS[:, c, :], SH[0][:, c * UTOK:(c + 1) * UTOK], ACT.Silu,
                                                 bias=BS[:, 0, c:c + 1]).then_inc(sgs_done, 1)
                    if later(it, j, 1):
                        if later(it, j, 3):
                            b, turn = slot(j - 3)
                            act.wait_ge(sent[b], 64 * (it + turn + 1))
                        for p in range(2):
                            act.wait_ge(yb_done, 2 * n - 1 + p)
                            for a in range(2):
                                nc.scalar.activation(YW[:, (j - 1) % 2, p, a, :], YB[:, p, a, :], ACT.Copy,
                                                     scale=XB[:, (j - 1) % SLOTS, p, a, DIM:DIM + 1]).then_inc(yw_done, 1)

                run_b(act, step)

            @block.vector
            def _(dve):
                own_v = Links(dve, meta_own)

                def chain(ins):
                    own_v.done(ins)
                    own_v.wait()

                dve.wait_ge(count_ready, 1)
                chain(nc.vector.tensor_copy(CI[:, :], PS[7][0:1, 0:EXPERTS]))
                chain(nc.vector.tensor_scalar(NTI[:, :], CI[:, :], float(ETILE - 1), None, ALU.add))
                chain(nc.vector.tensor_scalar(NTI[:, :], NTI[:, :], ETILE.bit_length() - 1, None, ALU.arith_shift_right))
                chain(nc.vector.tensor_copy(NTF[:, :], NTI[:, :]))
                chain(nc.vector.tensor_tensor(CUM8[:, :, :], spread(NTF[:, :], 1, EXPERTS),
                                              tri8[0:1, :].rearrange("p (a b) -> p a b", a=EXPERTS), ALU.mult))
                chain(nc.vector.reduce_sum(INC[:, :], CUM8[:, :, :], AX.X))
                chain(nc.vector.tensor_scalar(SKIP[:, :], NTF[:, :], -float(ETILE), float(REGION), ALU.mult, ALU.add))
                chain(nc.vector.tensor_tensor(PAST[:, :, :], spread(iota_tiles[0:1, :], 2, EXPERTS), spread(INC[:, :], 1, ETILES), ALU.is_ge))
                chain(nc.vector.tensor_tensor(PSKIP[:, :, :], PAST[:, :, :], spread(SKIP[:, :], 1, ETILES), ALU.mult))
                chain(nc.vector.reduce_sum(EOF[:, :], PAST[:, :, :], AX.X))
                chain(nc.vector.reduce_sum(ROF[:, :], PSKIP[:, :, :], AX.X))
                chain(nc.vector.scalar_tensor_tensor(out=RO2[:, :], in0=iota_tiles[0:1, :], scalar=float(ETILE), in1=ROF[:, :],
                                                     op0=ALU.mult, op1=ALU.add))
                chain(nc.vector.tensor_copy(META[:, :, 0], RO2[:, :]))
                nc.vector.tensor_scalar(META[:, :, 1], EOF[:, :], float(EXPERTS - 1), None, ALU.min).then_inc(meta_done, 1)

                def step(it, j):
                    n = SLOTS * it + j
                    if is_step(it, j):
                        for p in range(2):
                            dve.wait_ge(sg_done, 2 * n + p + 1)
                            nc.vector.scalar_tensor_tensor(out=HT[:, j % 2, p, :], in0=H[p][:, ETILE:2 * ETILE], scalar=WB[:, j % SLOTS, p, 385:386],
                                                           in1=SG[:, p, :], op0=ALU.add, op1=ALU.mult).then_inc(ht_done, 1)
                    if has_shared(it, j):
                        for c in range(2):
                            dve.wait_ge(sgs_done, 2 * n + c + 1)
                            nc.vector.scalar_tensor_tensor(out=HS[:, j % 2, c, :], in0=SH[1][:, c * UTOK:(c + 1) * UTOK], scalar=BS[:, 1, c:c + 1],
                                                           in1=SGS[:, c, :], op0=ALU.add, op1=ALU.mult).then_inc(hs_done, 1)
                    if is_step(it, j + 1):
                        dve.wait_ge(tx_ready, n + 2)
                        nc.vector.tensor_copy(XTB[:, (j + 1) % 2, :], TX[:, :]).then_inc(tx_out, 1)
                    if later(it, j, 1):
                        for p in range(2):
                            dve.wait_ge(y_ready, 2 * n - 1 + p)
                            if later(it, j, 2):
                                dve.wait_ge(yw_done, 4 * n - 6 + 2 * p)
                            nc.vector.tensor_tensor(YB[:, p, :, :], YP[p][:, 0:2 * DIM].rearrange("p (a d) -> p a d", a=2),
                                                    spread(WB[:, (j - 1) % SLOTS, p, 386:386 + DIM], 1, 2), ALU.add).then_inc(yb_done, 1)
                        if has_shared(it, j - 1):
                            dve.wait_ge(z_ready, n)
                            if later(it, j, 2):
                                dve.wait_ge(x_done, n - 1)
                            nc.vector.tensor_tensor(ZB[:, :, :], ZP[:, 0:UT * DIM].rearrange("p (t d) -> p t d", t=UT),
                                                    spread(BS2[:, :], 1, UT), ALU.add).then_inc(zb_done, 1)
                            dve.wait_ge(zb_done, n)
                            here = X[:, bass.ds((n - 1) * UT, UT), :]
                            nc.vector.scalar_tensor_tensor(out=here, in0=ZB[:, :, :], scalar=TG[:, 1:2], in1=here, op0=ALU.mult,
                                                           op1=ALU.add).then_inc(x_done, 1)

                run_b(dve, step)

            @block.gpsimd
            def _(pool):
                def step(it, j):
                    if not later(it, j, 1):
                        return
                    b, turn = slot(j - 1)
                    n = SLOTS * it + j - 1
                    for p in range(2):
                        for a in range(2):
                            wait_apart(pool, (yw_done, 4 * n + 2 * p + a + 1))
                            nc.gpsimd.indirect_dma_start(
                                results[:, :], bass.IndirectOffsetOnAxis(ap=XB[:, b, p, a, DIM + 1:DIM + 2].bitcast(i32), axis=0),
                                YW[:, b % 2, p, a, :], None).then_inc(sent[b], 16)

                run_b(pool, step)
                for b in range(SLOTS):
                    pool.wait_ge(sent[b], 64 * ((STEPS - b + SLOTS - 1) // SLOTS))

        with ExitStack() as own:
            NB = 4
            YC = own.enter_context(nc.sbuf_tensor("YC", [128, NB, TOPK, CG, DIM], f32))
            YSUM = own.enter_context(nc.sbuf_tensor("YSUM", [128, NB, CG, DIM], f32))
            y_in = [sem(f"y_in{b}") for b in range(NB)]
            ysum_done, out_ready, stored = sem("ysum_done"), sem("out_ready"), sem("stored")
            block = own.enter_context(nc.Block())
            y_tiles = results[0:TOPK * TOKENS, :].rearrange("(s a p) d -> s p a d", s=TOPK, p=128)
            CSTEPS = TILES // CG

            def run_c(engine, body):
                for b in range(NB):
                    body(0, b, True)
                with engine.Fori(1, CSTEPS // NB) as it:
                    for b in range(NB):
                        body(it, b, False)

            @block.sync
            def _(sp):
                def body(it, b, first):
                    n = it * NB + b
                    if not first:
                        sp.wait_ge(ysum_done, n - NB + 1)
                    for s in range(TOPK):
                        sp.dma_start(YC[:, b, s, :, :], y_tiles[s, :, bass.ds(n * CG, CG), :]).then_inc(y_in[b], 16)

                run_c(sp, body)

            @block.vector
            def _(dve):
                def body(it, b, first):
                    n = it * NB + b
                    dve.wait_ge(y_in[b], 32 * (it + 1))
                    if not first:
                        dve.wait_ge(out_ready, n - NB + 1)
                    nc.vector.tensor_tensor(YSUM[:, b, :, :], YC[:, b, 0, :, :], YC[:, b, 1, :, :], ALU.add).then_inc(ysum_done, 1)
                    dve.wait_ge(ysum_done, n + 1)
                    here = X[:, bass.ds(n * CG, CG), :]
                    nc.vector.tensor_tensor(here, here, YSUM[:, b, :, :], ALU.add).then_inc(out_ready, 1)

                run_c(dve, body)

            @block.scalar
            def _(act):
                def body(it, b, first):
                    n = it * NB + b
                    act.wait_ge(out_ready, n + 1)
                    act.dma_start(out_tiles[:, bass.ds(n * CG, CG), :], X[:, bass.ds(n * CG, CG), :]).then_inc(stored, 16)

                run_c(act, body)
                act.wait_ge(stored, 16 * CSTEPS)


DVE_LINKS, POOL_LINKS = 27, 10

CONST_WIDTHS = (("ident", 128), ("hmask", HG), ("iota8", EXPERTS), ("base8", EXPERTS), ("tri8", EXPERTS * EXPERTS),
                ("iota_tiles", ETILES), ("tri", SEQ), ("rank", 128), ("ones", 128))


def shape_constants(np):
    p = np.arange(128)
    tables = {
        "ident": np.eye(128),
        "hmask": (p[:, None] // DK) % HG == np.arange(HG)[None, :],
        "iota8": np.tile(np.arange(EXPERTS), (128, 1)),
        "base8": np.tile(np.arange(EXPERTS) * REGION, (128, 1)),
        "tri8": np.tile((np.arange(EXPERTS)[None, :] <= np.arange(EXPERTS)[:, None]).reshape(1, -1), (128, 1)),
        "iota_tiles": np.tile(np.arange(ETILES), (128, 1)),
        "tri": np.where(np.arange(SEQ)[None, :] > p[:, None] % SEQ, NEG, 0.0),
        "rank": p[:, None] < p[None, :],
        "ones": np.ones((128, 128)),
    }
    consts = np.concatenate([tables[n].astype(np.float32) for n, _ in CONST_WIDTHS], axis=1)
    dest = np.arange(TOPK)[None, :, None] * TOKENS + np.arange(TILES)[None, None, :] * TILE + p[:, None, None]
    pad = np.zeros((PADS * ETILE, ROW), np.float32)
    pad.view(np.int32)[:, DIM + 1] = TOPK * TOKENS + np.arange(PADS * ETILE)
    return consts, dest.astype(np.int32), pad


def kernel(**inputs):
    import numpy as np
    import concourse.bacc as bacc
    from concourse.bass_utils import run_bass_kernel_spmd

    def w(name):
        return np.asarray(inputs["L0_ffn_" + name])

    consts, dest, pad = shape_constants(np)
    experts = np.concatenate([w("w1").transpose(0, 2, 1), w("w3").transpose(0, 2, 1), w("w2").transpose(0, 2, 1),
                              w("b1")[:, :, None], w("b3")[:, :, None],
                              np.broadcast_to(w("b2")[:, None, :], (EXPERTS, 128, DIM))], axis=2).reshape(EXPERTS * 128, WROW)
    arrays = {
        "x": inputs["x"], "ctx_in": inputs["ctx_1024"], "mask": inputs["mask_BxS2_ik0"], "g_xattn": inputs["g_xattn"],
        "g_ffn": inputs["g_ffn"], "wq": inputs["L0_xattn_WQ"], "wk": inputs["L0_xattn_WK"], "wv": inputs["L0_xattn_WV"],
        "wo": inputs["L0_xattn_WO"], "gate_w": w("gate_w").T, "gate_b": w("gate_b"), "experts": experts,
        "ws1": w("ws1").T, "bs1": w("bs1").reshape(SHARED // 128, 128).T, "ws3": w("ws3").T,
        "bs3": w("bs3").reshape(SHARED // 128, 128).T, "ws2": w("ws2").T, "bs2": w("bs2"),
        "consts": consts, "dest_rows": dest, "pad_rows": pad,
    }
    nc = bacc.Bacc("TRN2", target_bir_lowering=False, num_devices=1)
    feed, args = {}, {}
    for name, a in arrays.items():
        a = np.ascontiguousarray(np.asarray(a))
        feed["in_" + name] = a
        args[name] = nc.dram_tensor("in_" + name, a.shape, mybir.dt.from_np(a.dtype), kind="ExternalInput").ap()
    args["out"] = nc.dram_tensor("out", (BATCH, SEQ, DIM), mybir.dt.float32, kind="ExternalOutput").ap()
    build_program(nc, **args)
    r = run_bass_kernel_spmd(nc, [feed], core_ids=[0])
    return r.results[0]["out"]
```

```python
import concourse.bass as bass
from concourse import mybir
from contextlib import ExitStack

BATCH, SEQ, DIM, HEADS = 128, 64, 128, 16
DK = DIM // HEADS
EXPERTS, INTER, TOPK, SHARED = 8, 128, 2, 256
TOKENS = BATCH * SEQ
TILE = 128
TILES = TOKENS // TILE
UT = 2
UNITS = TILES // UT
UTOK = UT * TILE
GT = 2 * UT
GROUPS = TILES // GT
NEG = -1.0e30
EPS = 1e-5
SCORE_SCALE = float(DK) ** -0.5
HG = 4
VW = 2 * DK + 2

ROW = DIM + 2
ETILE = 256
REGION = TOKENS + ETILE
SPARE = EXPERTS * REGION
ETILES = (TOPK * TOKENS // ETILE + EXPERTS - 1 + 1) // 2 * 2
SPARES = ETILES - TOPK * TOKENS // ETILE
PADS = EXPERTS + SPARES
WROW = 3 * INTER + 2 + DIM
EARLY = 6
SLOTS = 8
CG = 4


class At:

    def __init__(self, it, k):
        self.n = it * 2 + k
        self.half = it + k // 2
        self.par = k % 2
        self.known = isinstance(it, int)

    def exists(self):
        return (not self.known) or 0 <= self.n < UNITS

    def later_than(self, m):
        return (not self.known) or self.n >= m


class Links:

    def __init__(self, engine, sem):
        self.engine, self.sem, self.count, self.base = engine, sem, 0, 0

    def done(self, ins):
        ins.then_inc(self.sem, 1)
        self.count += 1

    def wait(self, apart=False):
        if apart:
            wait_apart(self.engine, (self.sem, self.base + self.count))
        else:
            self.engine.wait_ge(self.sem, self.base + self.count)


def wait_apart(engine, *waits):
    for s, v in waits:
        engine.wait_ge(s, v)
    engine.nop(nofuse=True)


def spread(ap, axis, n):
    wide = ap.unsqueeze(axis)
    shape = list(wide.shape)
    shape[axis] = n
    return wide.broadcast_to(shape)


def build_program(nc, x, inputs_t, mask, attention_w, shared_w, experts, consts, dest_rows, pad_rows, out):
    f32, bf16, i32, u32 = mybir.dt.float32, mybir.dt.bfloat16, mybir.dt.int32, mybir.dt.uint32
    ALU, ACT, AX = mybir.AluOpType, mybir.ActivationFunctionType, mybir.AxisListType

    x_tiles = x.rearrange("(a r) s d -> (r s) a d", r=2)
    out_tiles = out.rearrange("(a r) s d -> (r s) a d", r=2)
    mask_rows = mask.rearrange("(a r) s -> a (r s)", r=2)

    routed = nc.dram_tensor("routed_rows", [SPARE + SPARES * ETILE, ROW], f32, kind="Internal").ap()
    results = nc.dram_tensor("expert_results", [TOPK * TOKENS + PADS * ETILE, DIM], f32, kind="Internal").ap()

    ctx = ExitStack()
    with ctx:
        def sb(name, shape, dt=f32):
            return ctx.enter_context(nc.sbuf_tensor(name, shape, dt))

        def sem(name):
            return ctx.enter_context(nc.semaphore(name))

        X = sb("X", [128, TILES, DIM])
        X2T = sb("X2T", [128, TOKENS])
        CST = sb("CST", [128, consts.shape[1]])
        DEST = sb("DEST", [128, TOPK, TILES], i32)
        at = {}
        pos = 0
        for name, width in CONST_WIDTHS:
            at[name] = CST[:, pos:pos + width]
            pos += width
        ident, hmask, iota8, base8, tri8, iota_tiles, CENTRE = (
            at[n] for n in ("ident", "hmask", "iota8", "base8", "tri8", "iota_tiles", "centre"))
        IB = sb("IB", [128, 128], bf16)
        TRI = sb("TRI", [128, SEQ], bf16)
        RANK = sb("RANK", [128, 128], bf16)
        ONES = sb("ONES", [128, 128], bf16)
        TG = sb("TG", [128, 2])
        NM = sb("NM", [128, TILES])
        CARRY = sb("CARRY", [128, GT + 1, EXPERTS], bf16)
        AW = sb("AW", [128, attention_w.shape[1]])
        WQ_IN, WK, WV, WO = (AW[:, i * DIM:(i + 1) * DIM] for i in range(4))
        GW, GB = AW[:, 4 * DIM:4 * DIM + EXPERTS], AW[:, 4 * DIM + EXPERTS:4 * DIM + 2 * EXPERTS]
        GATES = AW[:, 4 * DIM + 2 * EXPERTS:4 * DIM + 2 * EXPERTS + 2]
        WQ = sb("WQ", [128, DIM])
        SW = sb("SW", [128, shared_w.shape[1]])
        WS1, WS3 = SW[:, 0:SHARED], SW[:, SHARED:2 * SHARED]
        WS2 = SW[:, 2 * SHARED:2 * SHARED + SHARED // 128 * DIM].rearrange("p (c d) -> p c d", d=DIM)
        BS = SW[:, 2 * SHARED + SHARED // 128 * DIM:2 * SHARED + SHARED // 128 * DIM + 4].rearrange("p (w c) -> p w c", w=2)
        BS2 = SW[:, 2 * SHARED + SHARED // 128 * DIM + 4:]
        MI = sb("MI", [TILES, TILE], i32)
        MF = sb("MF", [TILES, TILE])
        loaded, dest_in, shared_in, mask_float, mask_turned, setup = (sem(n) for n in (
            "loaded", "dest_in", "shared_in", "mask_float", "mask_turned", "setup"))

        BANKS = ctx.enter_context(nc.psum_tensor("BANKS", [128, 8, 512], f32))
        PS = [BANKS[:, i, :] for i in range(8)]

        with ExitStack() as own:
            def sa(name, shape, dt=f32):
                return own.enter_context(nc.sbuf_tensor(name, shape, dt))

            ST1, ST2 = sa("ST1", [128, UT, 6]), sa("ST2", [128, UT, 6])
            MV1, MV2 = sa("MV1", [128, UT, 2]), sa("MV2", [128, UT, 2])
            RS1, RS2, VE1, VE2 = (sa(n, [128, UT]) for n in ("RS1", "RS2", "VE1", "VE2"))
            RQ = sa("RQ", [128, 2, UT])
            HALFNEG, EPSV = sa("HALFNEG", [128, UT]), sa("EPSV", [128, UT])
            XCT = sa("XCT", [128, 2, 2, UTOK])
            QT = sa("QT", [128, 2 * UT, SEQ])
            KB = sa("KB", [128, 2 * UT, HG, SEQ])
            MX = sa("MX", [128, HG, 8])
            P = sa("P", [128, 2, HG, 512])
            PT = sa("PT", [128, 2, 512])
            VX = sa("VX", [128, 2, 2, UT, HEADS // 2, VW])
            R = sa("R", [128, UT * 8, 2])
            A = sa("A", [128, UT, DIM])
            AT = sa("AT", [128, UTOK])
            X2 = sa("X2", [128, GT, DIM])
            X2G = sa("X2G", [128, GT * TILE])
            LG = sa("LG", [128, GT, EXPERTS])
            M8 = sa("M8", [128, GT, 8])
            I8 = sa("I8", [128, GT, 8], u32)
            IF = sa("IF", [128, GT, TOPK])
            OH = sa("OH", [128, GT, TOPK, EXPERTS])
            OHS = sa("OHS", [128, GT, EXPERTS], bf16)
            NL = sa("NL", [128, GT, EXPERTS + TOPK])
            EX = sa("EX", [128, GT, EXPERTS + TOPK])
            Z, RZ = sa("Z", [128, GT]), sa("RZ", [128, GT])
            RB = sa("RB", [128, GT, EXPERTS])
            OP = sa("OP", [128, GT, TOPK, EXPERTS])
            PF = sa("PF", [128, GT, TOPK])
            IDX, IDX_LAST = sa("IDX", [128, TOPK, GT], i32), sa("IDX_LAST", [128, TOPK, GT], i32)
            STAGE = sa("STAGE", [128, TOPK, GT, ROW])
            STAGE_LAST = sa("STAGE_LAST", [128, TOPK, GT, ROW])

            S, T, M0, M1 = PS[0:4], PS[4:6], PS[6], PS[7]

            x_in = [sem("x_in0"), sem("x_in1")]
            t_in = [sem("t_in0"), sem("t_in1")]
            (buffers_set, stat1, rq_done, qk_ready, qk_out, v_ready, v_out, s_ready,
             sub_done, exp_done, t_ready, pt_out, pv_ready, norm_done, at_ready, at_out,
             wo_ready, resid, stat2, rs2_done, xn2_done, x2t_ready, x2t_out, x2t_saved, logits_ready, logits_used,
             nl_done, e_done, w_done, oh_done, rank_ready, rank_used, idx_done, stage_x, stage_dest, scattered,
             dve_own, pool_own) = (sem(n) for n in (
                 "buffers_set", "stat1", "rq_done", "qk_ready", "qk_out",
                 "v_ready", "v_out", "s_ready", "sub_done", "exp_done", "t_ready", "pt_out", "pv_ready", "norm_done",
                 "at_ready", "at_out", "wo_ready", "resid", "stat2", "rs2_done",
                 "xn2_done", "x2t_ready", "x2t_out", "x2t_saved", "logits_ready", "logits_used", "nl_done", "e_done",
                 "w_done", "oh_done", "rank_ready", "rank_used", "idx_done", "stage_x", "stage_dest", "scattered",
                 "dve_own", "pool_own"))

            CI, NTI, NTF = sa("CI", [1, EXPERTS], i32), sa("NTI", [1, EXPERTS], i32), sa("NTF", [1, EXPERTS])
            UPTO, INC, SKIP = sa("UPTO", [1, EXPERTS, EXPERTS]), sa("INC", [1, EXPERTS]), sa("SKIP", [1, EXPERTS])
            PAST = sa("PAST", [1, ETILES, EXPERTS])
            PSKIP = sa("PSKIP", [1, ETILES, EXPERTS])
            EOF = sa("EOF", [1, ETILES])
            ROF, RO2 = sa("ROF", [1, ETILES]), sa("RO2", [1, ETILES])
            META = sa("META", [1, ETILES, 2], i32)
            XB = sa("XB", [128, SLOTS, 2, 2, ROW])
            WB = sa("WB", [128, SLOTS, 2, WROW])
            XTB = sa("XTB", [128, 2, 2 * ETILE])
            SG = sa("SG", [128, 2, ETILE])
            HT = sa("HT", [128, 2, 2, ETILE])
            YB = sa("YB", [128, 2, 2, DIM])
            YW = sa("YW", [128, 2, 2, 2, DIM])
            SGS = sa("SGS", [128, 2, UTOK])
            HS = sa("HS", [128, 2, 2, UTOK])
            ZB = sa("ZB", [128, UT, DIM])
            TX, H, SH, ZP, YP = PS[0], PS[1:3], PS[3:5], PS[5], PS[6:8]
            SH_EARLY = (PS[0:2], PS[2:4])

            tiles_in = [sem(f"tiles_in{b}") for b in range(SLOTS)]
            sent = [sem(f"sent{b}") for b in range(SLOTS)]
            (count_ready, counts_known, meta_done, padded, tx_ready, tx_out, h_ready, sg_done, ht_done, y_ready, yb_done, yw_done,
             sh_ready, sgs_done, hs_done, z_ready, zb_done, x_done) = (sem(n) for n in (
                 "count_ready", "counts_known", "meta_done", "padded", "tx_ready", "tx_out", "h_ready", "sg_done", "ht_done", "y_ready",
                 "yb_done", "yw_done", "sh_ready", "sgs_done", "hs_done", "z_ready", "zb_done", "x_done"))

            block = own.enter_context(nc.Block())

            def around(it, k):
                return tuple(At(it, k + d) for d in (2, 1, 0, -1, -2, -3, -4))

            TRIPS = (UNITS - 6) // 2
            BEFORE = [(0, k) for k in range(-2, 6)]
            AFTER = [(TRIPS, k) for k in range(2, 10)]

            def run(engine, step, links=None, per_trip=0):
                for it, k in BEFORE:
                    step(it, k)
                first = links.count if links else 0
                with engine.Fori(2, TRIPS) as it:
                    if links:
                        links.base, links.count = first + (it - 2) * per_trip, 0
                    step(it, 2)
                    step(it, 3)
                    if links:
                        assert links.count == per_trip, (links.count, per_trip)
                if links:
                    links.base, links.count = 0, first + (TRIPS - 2) * per_trip
                for it, k in AFTER:
                    step(it, k)

            def last_group(w):
                return w.known and w.half == GROUPS - 1

            def stage_of(w):
                return STAGE_LAST if last_group(w) else STAGE

            def index_of(w):
                return IDX_LAST if last_group(w) else IDX

            def tiles_of(u):
                return bass.ds(u.n * UT, UT)

            def run_early(step):
                for m in range(EARLY + 1):
                    step(m)

            STEPS = ETILES // 2
            OWN = (0, 1, 2, 4, 5, 6)
            OWN_LAST = (1, 2)
            TURNS = STEPS // SLOTS
            assert UNITS - EARLY == TURNS * len(OWN) + len(OWN_LAST) and len(OWN_LAST) <= STEPS % SLOTS

            WITHIN = "the expert's number is capped, and the lists and spare tiles hold every row that follows from the counts"

            def run_experts(engine, step):
                for j in range(-1, SLOTS):
                    step(0, j)
                with engine.Fori(1, STEPS // SLOTS) as it:
                    for j in range(SLOTS):
                        step(it, j)
                for j in range(STEPS % SLOTS + 1):
                    step(STEPS // SLOTS, j)

            def is_step(it, j):
                return (not isinstance(it, int)) or 0 <= SLOTS * it + j < STEPS

            def own_steps(it):
                return OWN_LAST if isinstance(it, int) and it == TURNS else OWN

            def has_shared(it, j):
                return j in own_steps(it)

            def own_par(it, j):
                return own_steps(it).index(j) % 2

            def shared_unit(it, j):
                return EARLY + len(OWN) * it + own_steps(it).index(j)

            def later(it, j, m):
                return (not isinstance(it, int)) or SLOTS * it + j >= m

            def slot(j):
                return j % SLOTS, j // SLOTS

            @block.sync
            def _(sp):
                def load_x(u):
                    sp.dma_start(X[:, tiles_of(u), :], x_tiles[:, tiles_of(u), :]).then_inc(x_in[u.par], 16)

                def load_t(u):
                    sp.dma_start(XCT[:, u.par, :, :], inputs_t[:, bass.ds(u.n * 2 * UTOK, 2 * UTOK)]).then_inc(t_in[u.par], 16)

                sp.dma_start(CST[:, :], consts).then_inc(loaded, 16)
                load_t(At(0, 0))
                load_x(At(0, 0))
                load_t(At(0, 1))
                load_x(At(0, 1))
                sp.dma_start(DEST[:, :, :], dest_rows).then_inc(dest_in, 16)

                def step(it, k):
                    e, f, i, u, w, v, y = around(it, k)
                    f2 = At(it, k + 3)
                    if f2.exists() and f2.later_than(2):
                        sp.wait_ge(x_in[f.par], 16 * (f.half + 1))
                        load_x(f2)
                        sp.wait_ge(v_ready, f.n + 1)
                        load_t(f2)
                    if v.exists() and v.par:
                        sp.wait_ge(x2t_out, v.n + 1)
                        sp.dma_start(X2T[:, bass.ds(v.half * (GT * TILE), GT * TILE)], X2G[:, :]).then_inc(x2t_saved, 16)

                run(sp, step)
                sp.wait_ge(x2t_saved, 16 * GROUPS)

                sp.dma_start(routed[SPARE:, :], pad_rows[EXPERTS * ETILE:, :]).then_inc(padded, 16)
                sp.wait_ge(counts_known, 1)
                for e in range(EXPERTS):
                    count = sp.value_load(CI[0:1, e:e + 1], min_val=0, max_val=TOKENS)
                    sp.dma_start(routed[bass.ds(count + e * REGION, ETILE), :], pad_rows[e * ETILE:(e + 1) * ETILE, :]).then_inc(padded, 16)
                sp.wait_ge(meta_done, 1)

                def expert_step(it, j):
                    if not is_step(it, j):
                        return
                    b, turn = slot(j)
                    if later(it, j, SLOTS):
                        sp.wait_ge(sent[b], 64 * (it + turn))
                    _, places = nc.values_load_multi_w_load_instructions(
                        META[0:1, bass.ds((SLOTS * it + j) * 2, 2), :], engines=[mybir.EngineType.SP], min_val=0,
                        max_val=SPARE + (SPARES - 1) * ETILE, skip_runtime_bounds_check_because=WITHIN)
                    for p in range(2):
                        expert = nc.s_assert_within(places[2 * p + 1], 0, EXPERTS - 1, skip_runtime_bounds_check_because=WITHIN)
                        sp.dma_start(WB[:, b, p, :], experts[bass.ds(expert * 128, 128), :]).then_inc(tiles_in[b], 16)
                    if not later(it, j, 1):
                        sp.wait_ge(padded, 16 * (EXPERTS + 1))
                        sp.wait_ge(scattered, 16 * TOPK * GT * GROUPS)
                    for p in range(2):
                        rows = routed[bass.ds(places[2 * p], ETILE), :].rearrange("(p a) c -> p a c", a=2)
                        sp.dma_start(XB[:, b, p, :, :], rows).then_inc(tiles_in[b], 16)

                run_experts(sp, expert_step)

            @block.tensor
            def _(pe):
                pe.wait_ge(loaded, 48)
                nc.tensor.matmul(M1[:, 0:DIM], CENTRE, WQ_IN, start=True, stop=True)
                pe.wait_ge(mask_float, 1)
                nc.tensor.transpose(M1[:, DIM:DIM + TILES], MF[:, :], ident[0:TILES, 0:TILES]).then_inc(mask_turned, 1)
                pe.wait_ge(buffers_set, 3)
                pe.wait_ge(setup, 8)

                def scores(i, pair):
                    for g in pair:
                        nc.tensor.matmul(S[g][:, :], IB[:, :], spread(spread(TRI[:, :], 1, HG), 1, UT), start=True, stop=False,
                                         skip_group_check=True)
                    for t in range(UT):
                        for g in pair:
                            for b in range(2):
                                rows = slice(32 * g, 32 * g + 32)
                                last = nc.tensor.matmul(
                                    S[g][SEQ * b:SEQ * b + SEQ, t * HG * SEQ:(t + 1) * HG * SEQ], QT[rows, 2 * t + b, :],
                                    KB[rows, 2 * t + b, :, :], start=False, stop=(t == 1), tile_position=(32 * g, SEQ * b),
                                    skip_group_check=True)
                    last.then_inc(s_ready, 1)

                def turn_p(u, g):
                    if u.later_than(1) or g >= 2:
                        pe.wait_ge(pt_out, u.n * 4 + g - 1)
                    for c in range(4):
                        last = nc.tensor.transpose(T[g % 2][:, 128 * c:128 * c + 128],
                                                   P[:, u.par, g, 128 * c:128 * c + 128], ident)
                    last.then_inc(t_ready, 1)

                def p_v(u, g):
                    pe.wait_ge(pt_out, u.n * 4 + g + 1)
                    for t in range(UT):
                        for jp in range(2):
                            o = (t * 8 + g * 2 + jp) * VW
                            for b in range(2):
                                c = (2 * t + jp) * 128 + SEQ * b
                                last = nc.tensor.matmul(M0[SEQ * b:SEQ * b + SEQ, o:o + VW], PT[:, g % 2, c:c + SEQ],
                                                        VX[:, u.par, b, t, 2 * g + jp, :], start=True, stop=True,
                                                        tile_position=(0, SEQ * b))
                    return last

                def inner(banks, unit):
                    cols = X2T[:, bass.ds(unit * UTOK, UTOK)]
                    for c in range(2):
                        nc.tensor.matmul(banks[0][:, c * UTOK:(c + 1) * UTOK], WS1[:, c * 128:c * 128 + 128], cols, start=True, stop=True)
                    for c in range(2):
                        last = nc.tensor.matmul(banks[1][:, c * UTOK:(c + 1) * UTOK], WS3[:, c * 128:c * 128 + 128], cols,
                                                start=True, stop=True)
                    last.then_inc(sh_ready, 1)

                def inner_ahead(unit):
                    pe.wait_ge(sub_done, 2 * UNITS)
                    pe.wait_ge(x2t_saved, 16)
                    pe.wait_ge(shared_in, 16)
                    inner(SH_EARLY[unit], unit)

                def step(it, k):
                    e, f, i, u, w, v, y = around(it, k)
                    if i.exists():
                        pe.wait_ge(qk_out, 2 * (i.n + 1))
                        if i.later_than(1):
                            pe.wait_ge(sub_done, 2 * i.n - 1)
                        scores(i, (0, 1))
                    if w.exists():
                        pe.wait_ge(norm_done, w.n + 1)
                        if i.exists():
                            pe.wait_ge(v_out, 4 * (i.n + 1))
                        for t in range(UT):
                            last = nc.tensor.transpose(T[0][:, t * TILE:(t + 1) * TILE], A[:, t, :], ident)
                        last.then_inc(at_ready, 1)
                    if v.exists():
                        pe.wait_ge(xn2_done, v.n + 1)
                        if not w.exists():
                            pe.wait_ge(x2t_out, v.n)
                        for t in range(UT):
                            last = nc.tensor.transpose(T[0][:, UTOK + t * TILE:UTOK + (t + 1) * TILE], X2[:, v.par * UT + t, :], ident)
                        last.then_inc(x2t_ready, 1)
                    if i.exists():
                        if i.later_than(1):
                            pe.wait_ge(sub_done, 2 * i.n)
                        scores(i, (2, 3))
                    if v.exists():
                        pe.wait_ge(x2t_out, v.n + 1)
                        if not w.exists():
                            pe.wait_ge(resid, UNITS)
                            pe.wait_ge(logits_used, v.n)
                        for t in range(UT):
                            c = v.par * UTOK + t * TILE
                            last = nc.tensor.matmul(M0[:, t * EXPERTS:(t + 1) * EXPERTS], X2G[:, c:c + TILE], GW, start=True, stop=True)
                        last.then_inc(logits_ready, 1)
                        if v.known and v.n == UNITS - 1:
                            inner_ahead(1)
                    if y.exists() and y.par:
                        pe.wait_ge(oh_done, y.half + 1)
                        if not v.exists():
                            pe.wait_ge(logits_used, UNITS)
                        ranks = M0[:, GT * EXPERTS:2 * GT * EXPERTS]
                        nc.tensor.matmul(ranks, RANK[:, :], OHS[:, :, :], start=True, stop=False)
                        nc.tensor.matmul(ranks, ONES[:, :], CARRY[:, 0:GT, :], start=False, stop=True).then_inc(rank_ready, 1)
                    if w.exists():
                        pe.wait_ge(at_out, w.n + 1)
                        for t in range(UT):
                            last = nc.tensor.matmul(M0[:, UTOK + t * DIM:UTOK + (t + 1) * DIM], AT[:, t * TILE:(t + 1) * TILE], WO,
                                                    start=True, stop=True)
                        last.then_inc(wo_ready, 1)
                        if w.known and w.n == UNITS - 1:
                            inner_ahead(0)
                    if u.exists():
                        if v.exists():
                            pe.wait_ge(x2t_out, v.n + 1)
                        if i.exists() and not w.exists():
                            pe.wait_ge(v_out, 4 * (i.n + 1))
                        pe.wait_ge(exp_done, u.n * 2 + 1)
                        turn_p(u, 0)
                        turn_p(u, 1)
                    if f.exists():
                        pe.wait_ge(t_in[f.par], 16 * (f.half + 1))
                        if f.later_than(1):
                            pe.wait_ge(qk_out, 2 * f.n)
                        nc.tensor.matmul(M1[:, 0:UTOK], WQ[:, :], XCT[:, f.par, 0, :], start=True, stop=True)
                        nc.tensor.matmul(M1[:, UTOK:2 * UTOK], WK, XCT[:, f.par, 1, :], start=True, stop=True).then_inc(qk_ready, 1)
                    if u.exists():
                        pe.wait_ge(exp_done, u.n * 2 + 2)
                        if w.exists():
                            pe.wait_ge(resid, w.n + 1)
                        p_v(u, 0)
                        turn_p(u, 2)
                        p_v(u, 1)
                        turn_p(u, 3)
                        p_v(u, 2)
                    if f.exists():
                        if f.later_than(1) and not u.exists():
                            pe.wait_ge(v_out, 4 * f.n)
                        for t in range(UT):
                            last = nc.tensor.matmul(T[0][:, t * DIM:(t + 1) * DIM], XCT[:, f.par, 1, t * TILE:(t + 1) * TILE], WV,
                                                    start=True, stop=True)
                        last.then_inc(v_ready, 1)
                    if u.exists():
                        p_v(u, 3).then_inc(pv_ready, 1)

                run(pe, step)

                nc.tensor.matmul(M1[:, 0:EXPERTS], ONES[:, :], CARRY[:, GT, :], start=True, stop=True).then_inc(count_ready, 1)

                def outer(par):
                    for t in range(UT):
                        for c in range(2):
                            last = nc.tensor.matmul(ZP[:, t * DIM:(t + 1) * DIM], HS[:, par, c, t * TILE:(t + 1) * TILE],
                                                    WS2[:, c, :], start=(c == 0), stop=(c == 1))
                    last.then_inc(z_ready, 1)

                def early_step(m):
                    if 2 <= m < EARLY:
                        pe.wait_ge(hs_done, 2 * m - 2)
                        inner(SH_EARLY[m % 2], m)
                    if m >= 1:
                        pe.wait_ge(hs_done, 2 * m)
                        if m >= 2:
                            pe.wait_ge(zb_done, m - 1)
                        outer((m - 1) % 2)

                run_early(early_step)

                def expert_step(it, j):
                    n = SLOTS * it + j
                    if is_step(it, j):
                        pe.wait_ge(tx_out, n + 1)
                        if later(it, j, 1):
                            pe.wait_ge(ht_done, 2 * n)
                        for p in range(2):
                            cols = XTB[:, j % 2, p * ETILE:(p + 1) * ETILE]
                            nc.tensor.matmul(H[p][:, 0:ETILE], WB[:, j % SLOTS, p, 0:128], cols, start=True, stop=True)
                            nc.tensor.matmul(H[p][:, ETILE:2 * ETILE], WB[:, j % SLOTS, p, 128:256], cols, start=True,
                                             stop=True).then_inc(h_ready, 1)
                    if has_shared(it, j):
                        m = shared_unit(it, j)
                        pe.wait_ge(hs_done, 2 * m)
                        inner(SH, m)
                    if is_step(it, j + 1):
                        b, turn = slot(j + 1)
                        pe.wait_ge(tiles_in[b], 64 * (it + turn + 1))
                        if later(it, j, 0):
                            pe.wait_ge(tx_out, n + 1)
                        for p in range(2):
                            for a in range(2):
                                last = nc.tensor.transpose(TX[:, p * ETILE + a * 128:p * ETILE + a * 128 + 128],
                                                           XB[:, b, p, a, 0:DIM], ident)
                        last.then_inc(tx_ready, 1)
                    if later(it, j, 1):
                        for p in range(2):
                            pe.wait_ge(ht_done, 2 * n - 1 + p)
                            if later(it, j, 2):
                                pe.wait_ge(yb_done, 2 * n - 3 + p)
                            for a in range(2):
                                last = nc.tensor.matmul(YP[p][:, a * DIM:(a + 1) * DIM], HT[:, (j - 1) % 2, p, a * 128:a * 128 + 128],
                                                        WB[:, (j - 1) % SLOTS, p, 256:384], start=True, stop=True)
                            last.then_inc(y_ready, 1)
                        if has_shared(it, j - 1):
                            m = shared_unit(it, j - 1)
                            pe.wait_ge(hs_done, 2 * (m + 1))
                            pe.wait_ge(zb_done, m)
                            outer(own_par(it, j - 1))

                run_experts(pe, expert_step)

            @block.scalar
            def _(act):
                act.dma_start(AW[:, :], attention_w).then_inc(loaded, 16)
                act.dma_start(MI[:, :], mask_rows).then_inc(loaded, 16)
                act.dma_start(SW[:, :], shared_w).then_inc(shared_in, 16)
                act.wait_ge(loaded, 48)
                nc.scalar.activation(TG[:, :], GATES, ACT.Tanh).then_inc(setup, 1)
                act.wait_ge(setup, 8)

                def copy(dst, src):
                    return nc.scalar.activation(dst, src, ACT.Copy)

                def p_out(u, g):
                    act.wait_ge(t_ready, u.n * 4 + g + 1)
                    copy(PT[:, g % 2, :], T[g % 2][:, :]).then_inc(pt_out, 1)

                def soften(i, c):
                    act.wait_ge(sub_done, 2 * i.n + c + 1)
                    act.wait_ge(rq_done, i.n + 1)
                    for t in range(UT):
                        p = P[:, i.par, 2 * c:2 * c + 2, t * HG * SEQ:(t + 1) * HG * SEQ]
                        ins = nc.scalar.activation(p, p, ACT.Exp, scale=RQ[:, i.par, t:t + 1])
                    ins.then_inc(exp_done, 1)

                def masked_k(heads):
                    for h in heads:
                        ins = nc.scalar.activation(KB[:, :, h, :], M1[:, UTOK:2 * UTOK].rearrange("p (s k) -> p s k", k=SEQ),
                                                   ACT.Copy, scale=hmask[:, h:h + 1])
                    ins.then_inc(qk_out, 1)

                def step(it, k):
                    e, f, i, u, w, v, y = around(it, k)
                    if y.exists() and y.par:
                        act.wait_ge(nl_done, y.half + 1)
                        nc.scalar.activation(EX[:, :, :], NL[:, :, :], ACT.Exp).then_inc(e_done, 1)
                    if w.exists():
                        act.wait_ge(at_ready, w.n + 1)
                        if v.exists():
                            act.wait_ge(x2t_ready, v.n + 1)
                        copy(AT[:, :], T[0][:, 0:UTOK]).then_inc(at_out, 1)
                    if v.exists():
                        act.wait_ge(x2t_ready, v.n + 1)
                        if not v.par and v.later_than(2):
                            act.wait_ge(x2t_saved, 16 * v.half)
                        copy(X2G[:, v.par * UTOK:(v.par + 1) * UTOK], T[0][:, UTOK:2 * UTOK]).then_inc(x2t_out, 1)
                    if i.exists():
                        soften(i, 0)
                    if u.exists():
                        p_out(u, 0)
                        p_out(u, 1)
                    if f.exists():
                        act.wait_ge(qk_ready, f.n + 1)
                        copy(QT[:, :, :], M1[:, 0:UTOK])
                    if u.exists():
                        p_out(u, 2)
                    if f.exists():
                        masked_k((0, 1))
                    if u.exists():
                        p_out(u, 3)
                    if f.exists():
                        masked_k((2, 3))
                        act.wait_ge(v_ready, f.n + 1)
                        if u.exists():
                            act.wait_ge(pv_ready, u.n + 1)
                        for b in range(2):
                            for j in range(2):
                                copy(VX[SEQ * j:SEQ * j + SEQ, f.par, b, :, :, DK * j:DK * j + DK],
                                     T[0][SEQ * b:SEQ * b + SEQ, 0:UT * DIM].rearrange("p (t h c) -> p t h c", t=UT, c=16)
                                     [:, :, :, DK * j:DK * j + DK]).then_inc(v_out, 1)
                    if v.exists() and v.par:
                        act.wait_ge(xn2_done, v.n + 1)
                        if v.later_than(2) and not last_group(v):
                            act.wait_ge(scattered, 16 * TOPK * GT * v.half)
                        copy(stage_of(v)[:, :, :, 0:DIM], spread(X2[:, :, :], 1, TOPK)).then_inc(stage_x, 1)
                    if i.exists():
                        soften(i, 1)

                run(act, step)

                def gate(banks, m):
                    act.wait_ge(sh_ready, m + 1)
                    for c in range(2):
                        nc.scalar.activation(SGS[:, c, :], banks[0][:, c * UTOK:(c + 1) * UTOK], ACT.Silu,
                                             bias=BS[:, 0, c:c + 1]).then_inc(sgs_done, 1)

                def early_step(m):
                    if m < EARLY:
                        if m >= 1:
                            act.wait_ge(hs_done, 2 * m)
                        gate(SH_EARLY[m % 2], m)

                run_early(early_step)

                def expert_step(it, j):
                    n = SLOTS * it + j
                    if is_step(it, j):
                        for p in range(2):
                            act.wait_ge(h_ready, 2 * n + p + 1)
                            nc.scalar.activation(SG[:, p, :], H[p][:, 0:ETILE], ACT.Silu, bias=WB[:, j % SLOTS, p, 384:385]).then_inc(sg_done, 1)
                    if has_shared(it, j):
                        gate(SH, shared_unit(it, j))
                    if later(it, j, 1):
                        if later(it, j, 3):
                            b, turn = slot(j - 3)
                            act.wait_ge(sent[b], 64 * (it + turn + 1))
                        for p in range(2):
                            act.wait_ge(yb_done, 2 * n - 1 + p)
                            for a in range(2):
                                nc.scalar.activation(YW[:, (j - 1) % 2, p, a, :], YB[:, p, a, :], ACT.Copy,
                                                     scale=XB[:, (j - 1) % SLOTS, p, a, DIM:DIM + 1]).then_inc(yw_done, 1)

                run_experts(act, expert_step)

            @block.vector
            def _(dve):
                own_v = Links(dve, dve_own)
                for p in range(2):
                    own_v.done(nc.vector.memset(VX[:, p, :, :, :, :].rearrange("p b t h c -> p (b t h c)"), 0.0))
                own_v.wait()
                for j in range(2):
                    for p in range(2):
                        ins = nc.vector.memset(VX[SEQ * j:SEQ * j + SEQ, p, :, :, :, 2 * DK + j:2 * DK + j + 1].rearrange("p b t h c -> p (b t h) c"), 1.0)
                        if p == 1:
                            ins.then_inc(buffers_set, 1)
                        else:
                            own_v.done(ins)
                own_v.wait()
                nc.vector.memset(EPSV[:, :], EPS)
                nc.vector.memset(HALFNEG[:, :], -0.5).then_inc(buffers_set, 1)
                nc.vector.memset(CARRY[:, :, :], 0.0).then_inc(setup, 1)
                dve.wait_ge(loaded, 48)
                nc.vector.tensor_scalar(MF[:, :], MI[:, :], 0.0, None, ALU.is_equal).then_inc(mask_float, 1)
                for dst, name in ((IB, "ident"), (TRI, "tri"), (RANK, "rank"), (ONES, "ones")):
                    nc.vector.tensor_copy(dst[:, :], at[name]).then_inc(setup, 1)
                dve.wait_ge(mask_turned, 1)
                nc.vector.tensor_copy(WQ[:, :], M1[:, 0:DIM]).then_inc(setup, 1)
                nc.vector.tensor_scalar(NM[:, :], M1[:, DIM:DIM + TILES], SCORE_SCALE, None, ALU.mult).then_inc(setup, 1)

                def statistics(rows, st, mv, done):
                    for t in range(UT):
                        last = nc.vector.bn_stats(st[:, t, :], rows[t])
                    own_v.done(last)
                    own_v.wait(apart=True)
                    for t in range(UT):
                        last = nc.vector.bn_aggr(mv[:, t, :], st[:, t, :])
                    last.then_inc(done, 1)

                def take_logits(v):
                    dve.wait_ge(logits_ready, v.n + 1)
                    nc.vector.tensor_tensor(LG[:, v.par * UT:(v.par + 1) * UT, :], M0[:, 0:UT * EXPERTS].rearrange("p (t e) -> p t e", t=UT),
                                            spread(GB, 1, UT), ALU.add).then_inc(logits_used, 1)

                def choose(w):
                    g1 = w.half + 1
                    wait_apart(dve, (logits_used, 2 * g1))
                    for t in range(GT):
                        ins = nc.vector.max(M8[:, t, :], LG[:, t, :])
                    own_v.done(ins)
                    own_v.wait()
                    nc.vector.tensor_tensor(NL[:, :, 0:EXPERTS], LG[:, :, :], M8[:, :, 0:1].broadcast_to([128, GT, EXPERTS]),
                                            ALU.subtract)
                    nc.vector.tensor_tensor(NL[:, :, EXPERTS:], M8[:, :, 0:TOPK], M8[:, :, 0:1].broadcast_to([128, GT, TOPK]),
                                            ALU.subtract).then_inc(nl_done, 1)
                    for t in range(GT):
                        ins = nc.vector.max_index(I8[:, t, :], M8[:, t, :], LG[:, t, :])
                    own_v.done(ins)
                    own_v.wait()
                    own_v.done(nc.vector.tensor_copy(IF[:, :, :], I8[:, :, 0:TOPK]))
                    own_v.wait()
                    own_v.done(nc.vector.tensor_tensor(OH[:, :, :, :], spread(spread(iota8, 1, TOPK), 1, GT),
                                                       spread(IF[:, :, :], 3, EXPERTS), ALU.is_equal))
                    own_v.wait()
                    own_v.done(nc.vector.tensor_tensor(OHS[:, :, :], OH[:, :, 0, :], OH[:, :, 1, :], ALU.add))
                    own_v.wait()
                    for t in range(GT):
                        ins = nc.vector.tensor_tensor(CARRY[:, t + 1, :], CARRY[:, t, :], OHS[:, t, :], ALU.add)
                        if t < GT - 1:
                            own_v.done(ins)
                            own_v.wait()
                    ins.then_inc(oh_done, 1)

                def take_ranks(w):
                    g1 = w.half + 1
                    dve.wait_ge(rank_ready, g1)
                    nc.vector.tensor_tensor(RB[:, :, :], M0[:, GT * EXPERTS:2 * GT * EXPERTS].rearrange("p (t e) -> p t e", t=GT),
                                            spread(base8, 1, GT), ALU.add).then_inc(rank_used, 1)

                def place(w):
                    g1 = w.half + 1
                    dve.wait_ge(e_done, g1)
                    own_v.done(nc.vector.reduce_sum(Z[:, :], EX[:, :, 0:EXPERTS], AX.X))
                    own_v.wait()
                    own_v.done(nc.vector.reciprocal(RZ[:, :], Z[:, :]))
                    own_v.wait()
                    if w.later_than(2) and not last_group(w):
                        dve.wait_ge(scattered, 16 * TOPK * GT * w.half)
                    nc.vector.scalar_tensor_tensor(
                        out=stage_of(w)[:, :, :, DIM].rearrange("p s t -> p t s"), in0=EX[:, :, EXPERTS:], scalar=TG[:, 1:2],
                        in1=spread(RZ[:, :], 2, TOPK), op0=ALU.mult, op1=ALU.mult).then_inc(w_done, 1)
                    own_v.done(nc.vector.tensor_copy(CARRY[:, 0, :], CARRY[:, GT, :]))
                    dve.wait_ge(rank_used, g1)
                    own_v.done(nc.vector.tensor_tensor(OP[:, :, :, :], OH[:, :, :, :], spread(RB[:, :, :], 2, TOPK), ALU.mult))
                    own_v.wait()
                    own_v.done(nc.vector.reduce_sum(PF[:, :, :], OP[:, :, :, :], AX.X))
                    own_v.wait()
                    nc.vector.tensor_copy(index_of(w)[:, :, :].rearrange("p s t -> p t s"), PF[:, :, :]).then_inc(idx_done, 1)

                def softmax_shift(i, c):
                    banks = BANKS[:, 2 * c:2 * c + 2, :].rearrange("p g (c k) -> p g c k", c=8)
                    own_v.done(nc.vector.tensor_reduce(out=MX[:, 2 * c:2 * c + 2, :], in_=banks, axis=AX.X, op=ALU.max))
                    own_v.wait()
                    nc.vector.tensor_tensor(P[:, i.par, 2 * c:2 * c + 2, :].rearrange("p g (c k) -> p g c k", c=8), banks,
                                            spread(MX[:, 2 * c:2 * c + 2, :], 3, SEQ), ALU.subtract).then_inc(sub_done, 1)

                def chain(ins):
                    own_v.done(ins)
                    own_v.wait()

                def count_tiles():
                    dve.wait_ge(counts_known, 1)
                    chain(nc.vector.tensor_scalar(NTI[:, :], CI[:, :], float(ETILE - 1), None, ALU.add))
                    chain(nc.vector.tensor_scalar(NTI[:, :], NTI[:, :], ETILE.bit_length() - 1, None, ALU.arith_shift_right))
                    chain(nc.vector.tensor_copy(NTF[:, :], NTI[:, :]))
                    chain(nc.vector.tensor_tensor(UPTO[:, :, :], spread(NTF[:, :], 1, EXPERTS),
                                                  tri8[0:1, :].rearrange("p (a b) -> p a b", a=EXPERTS), ALU.mult))
                    chain(nc.vector.reduce_sum(INC[:, :], UPTO[:, :, :], AX.X))
                    chain(nc.vector.tensor_scalar(SKIP[:, :], NTF[:, :], -float(ETILE), float(REGION), ALU.mult, ALU.add))

                def find_experts():
                    chain(nc.vector.tensor_tensor(PAST[:, :, :], spread(iota_tiles[0:1, :], 2, EXPERTS), spread(INC[:, :], 1, ETILES), ALU.is_ge))
                    chain(nc.vector.tensor_tensor(PSKIP[:, :, :], PAST[:, :, :], spread(SKIP[:, :], 1, ETILES), ALU.mult))

                def list_tiles():
                    chain(nc.vector.reduce_sum(EOF[:, :], PAST[:, :, :], AX.X))
                    chain(nc.vector.reduce_sum(ROF[:, :], PSKIP[:, :, :], AX.X))
                    chain(nc.vector.scalar_tensor_tensor(out=RO2[:, :], in0=iota_tiles[0:1, :], scalar=float(ETILE), in1=ROF[:, :],
                                                         op0=ALU.mult, op1=ALU.add))
                    chain(nc.vector.tensor_copy(META[:, :, 0], RO2[:, :]))
                    nc.vector.tensor_scalar(META[:, :, 1], EOF[:, :], float(EXPERTS - 1), None, ALU.min).then_inc(meta_done, 1)

                LISTING = (count_tiles, find_experts, list_tiles)

                def step(it, k):
                    e, f, i, u, w, v, y = around(it, k)
                    if i.exists():
                        dve.wait_ge(s_ready, 2 * i.n + 1)
                        softmax_shift(i, 0)
                    if f.exists():
                        wait_apart(dve, (x_in[f.par], 16 * (f.half + 1)), *[(rq_done, f.n)] * f.later_than(1))
                        statistics([X[:, bass.ds(f.n * UT + t, 1), :] for t in range(UT)], ST1, MV1, stat1)
                    if w.exists():
                        dve.wait_ge(wo_ready, w.n + 1)
                    if v.exists():
                        take_logits(v)
                    if y.exists() and y.par:
                        take_ranks(y)
                        if last_group(y):
                            dve.wait_ge(count_ready, 1)
                            nc.vector.tensor_copy(CI[:, :], M1[0:1, 0:EXPERTS]).then_inc(counts_known, 1)
                    if w.exists():
                        dve.wait_ge(wo_ready, w.n + 1)
                        here = X[:, tiles_of(w), :]
                        nc.vector.scalar_tensor_tensor(
                            out=here, in0=M0[:, UTOK:UTOK + UT * DIM].rearrange("p (t d) -> p t d", t=UT), scalar=TG[:, 0:1],
                            in1=here, op0=ALU.mult, op1=ALU.add).then_inc(resid, 1)
                        wait_apart(dve, (resid, w.n + 1))
                        statistics([X[:, bass.ds(w.n * UT + t, 1), :] for t in range(UT)], ST2, MV2, stat2)
                    if i.exists():
                        dve.wait_ge(s_ready, 2 * i.n + 2)
                        softmax_shift(i, 1)
                    if v.exists() and v.par:
                        choose(v)
                    if y.exists() and y.par:
                        place(y)
                    if u.exists():
                        dve.wait_ge(pv_ready, u.n + 1)
                        if u.later_than(1):
                            dve.wait_ge(at_ready, u.n)
                        heads = M0[:, 0:UT * 8 * VW].rearrange("p (h c) -> p h c", c=VW)
                        own_v.done(nc.vector.reciprocal(R[:, :, :], heads[:, :, 2 * DK:VW]))
                        own_v.wait()
                        nc.vector.tensor_tensor(
                            A[:, :, :].rearrange("p t (h j c) -> p (t h) j c", j=2, c=DK),
                            heads[:, :, 0:2 * DK].rearrange("p h (j c) -> p h j c", j=2), spread(R[:, :, :], 3, DK),
                            ALU.mult).then_inc(norm_done, 1)
                    if w.exists():
                        dve.wait_ge(rs2_done, w.n + 1)
                        if not w.par and w.later_than(2):
                            dve.wait_ge(stage_x, w.half)
                            dve.wait_ge(x2t_ready, w.n)
                        for t in range(UT):
                            ins = nc.vector.tensor_scalar(
                                X2[:, w.par * UT + t, :], X[:, bass.ds(w.n * UT + t, 1), :], MV2[:, t, 0:1], RS2[:, t:t + 1],
                                ALU.subtract, ALU.mult)
                        ins.then_inc(xn2_done, 1)

                run(dve, step, own_v, DVE_LINKS)

                def shared_inner(banks, m, par):
                    for c in range(2):
                        dve.wait_ge(sgs_done, 2 * m + c + 1)
                        nc.vector.scalar_tensor_tensor(out=HS[:, par, c, :], in0=banks[1][:, c * UTOK:(c + 1) * UTOK], scalar=BS[:, 1, c:c + 1],
                                                       in1=SGS[:, c, :], op0=ALU.add, op1=ALU.mult).then_inc(hs_done, 1)

                def shared_result(m, has_former):
                    dve.wait_ge(z_ready, m + 1)
                    if has_former:
                        dve.wait_ge(x_done, m)
                    nc.vector.tensor_tensor(ZB[:, :, :], ZP[:, 0:UT * DIM].rearrange("p (t d) -> p t d", t=UT),
                                            spread(BS2, 1, UT), ALU.add).then_inc(zb_done, 1)
                    dve.wait_ge(zb_done, m + 1)
                    here = X[:, bass.ds(m * UT, UT), :]
                    nc.vector.scalar_tensor_tensor(out=here, in0=ZB[:, :, :], scalar=TG[:, 1:2], in1=here, op0=ALU.mult,
                                                   op1=ALU.add).then_inc(x_done, 1)

                def early_step(m):
                    if m < EARLY:
                        if m >= 2:
                            dve.wait_ge(z_ready, m - 1)
                        shared_inner(SH_EARLY[m % 2], m, m % 2)
                    if m >= 1:
                        shared_result(m - 1, m >= 2)
                    if m < len(LISTING):
                        LISTING[m]()

                run_early(early_step)

                def expert_step(it, j):
                    n = SLOTS * it + j
                    if is_step(it, j):
                        for p in range(2):
                            dve.wait_ge(sg_done, 2 * n + p + 1)
                            nc.vector.scalar_tensor_tensor(out=HT[:, j % 2, p, :], in0=H[p][:, ETILE:2 * ETILE], scalar=WB[:, j % SLOTS, p, 385:386],
                                                           in1=SG[:, p, :], op0=ALU.add, op1=ALU.mult).then_inc(ht_done, 1)
                    if has_shared(it, j):
                        shared_inner(SH, shared_unit(it, j), own_par(it, j))
                    if is_step(it, j + 1):
                        dve.wait_ge(tx_ready, n + 2)
                        nc.vector.tensor_copy(XTB[:, (j + 1) % 2, :], TX[:, :]).then_inc(tx_out, 1)
                    if later(it, j, 1):
                        for p in range(2):
                            dve.wait_ge(y_ready, 2 * n - 1 + p)
                            if later(it, j, 2):
                                dve.wait_ge(yw_done, 4 * n - 6 + 2 * p)
                            nc.vector.tensor_tensor(YB[:, p, :, :], YP[p][:, 0:2 * DIM].rearrange("p (a d) -> p a d", a=2),
                                                    spread(WB[:, (j - 1) % SLOTS, p, 386:386 + DIM], 1, 2), ALU.add).then_inc(yb_done, 1)
                        if has_shared(it, j - 1):
                            shared_result(shared_unit(it, j - 1), True)

                run_experts(dve, expert_step)

            @block.gpsimd
            def _(pool):
                own_p = Links(pool, pool_own)
                pool.wait_ge(dest_in, 16)
                pool.wait_ge(buffers_set, 3)
                pool.wait_ge(setup, 8)

                def rstd(rs, ve, mv):
                    own_p.done(nc.gpsimd.tensor_tensor(ve[:, :], mv[:, :, 1], EPSV[:, :], ALU.add))
                    own_p.wait()
                    return nc.gpsimd.tensor_tensor(rs[:, :], ve[:, :], HALFNEG[:, :], ALU.pow)

                def scatter(y, s):
                    for t in range(GT):
                        nc.gpsimd.indirect_dma_start(
                            routed[:, :], bass.IndirectOffsetOnAxis(ap=index_of(y)[:, s, t:t + 1], axis=0),
                            stage_of(y)[:, s, t, :], None).then_inc(scattered, 16)

                def step(it, k):
                    e, f, i, u, w, v, y = around(it, k)
                    placing = y.exists() and y.par
                    if f.exists():
                        pool.wait_ge(stat1, f.n + 1)
                        own_p.done(rstd(RS1, VE1, MV1))
                        wait_apart(pool, *[(exp_done, 2 * f.n - 2)] * f.later_than(2))
                        own_p.wait(apart=True)
                        nc.gpsimd.tensor_tensor(RQ[:, f.par, :], RS1[:, :], NM[:, tiles_of(f)], ALU.mult).then_inc(rq_done, 1)
                    if w.exists():
                        pool.wait_ge(stat2, w.n + 1)
                        rstd(RS2, VE2, MV2).then_inc(rs2_done, 1)
                    if placing:
                        if y.later_than(2) and not last_group(y):
                            pool.wait_ge(scattered, 16 * TOPK * GT * y.half)
                        nc.gpsimd.tensor_copy(stage_of(y)[:, :, :, DIM + 1].bitcast(i32),
                                              DEST[:, :, bass.ds(y.half * GT, GT)]).then_inc(stage_dest, 1)
                        wait_apart(pool, (stage_dest, y.half + 1), (stage_x, y.half + 1), (w_done, y.half + 1),
                                   (idx_done, y.half + 1))
                        scatter(y, 0)
                        scatter(y, 1)

                run(pool, step, own_p, POOL_LINKS)

                def expert_step(it, j):
                    if not later(it, j, 1):
                        return
                    b, turn = slot(j - 1)
                    n = SLOTS * it + j - 1
                    for p in range(2):
                        for a in range(2):
                            wait_apart(pool, (yw_done, 4 * n + 2 * p + a + 1))
                            nc.gpsimd.indirect_dma_start(
                                results[:, :], bass.IndirectOffsetOnAxis(ap=XB[:, b, p, a, DIM + 1:DIM + 2].bitcast(i32), axis=0),
                                YW[:, b % 2, p, a, :], None).then_inc(sent[b], 16)

                run_experts(pool, expert_step)
                for b in range(SLOTS):
                    pool.wait_ge(sent[b], 64 * ((STEPS - b + SLOTS - 1) // SLOTS))

        with ExitStack() as own:
            NB = 4
            YC = own.enter_context(nc.sbuf_tensor("YC", [128, NB, TOPK, CG, DIM], f32))
            YSUM = own.enter_context(nc.sbuf_tensor("YSUM", [128, NB, CG, DIM], f32))
            y_in = [sem(f"y_in{b}") for b in range(NB)]
            ysum_done, out_ready, stored = sem("ysum_done"), sem("out_ready"), sem("stored")
            block = own.enter_context(nc.Block())
            y_tiles = results[0:TOPK * TOKENS, :].rearrange("(s p a) d -> s p a d", s=TOPK, p=128)
            CSTEPS = TILES // CG

            def run_out(engine, body):
                for b in range(NB):
                    body(0, b, True)
                with engine.Fori(1, CSTEPS // NB) as it:
                    for b in range(NB):
                        body(it, b, False)

            @block.sync
            def _(sp):
                def body(it, b, first):
                    n = it * NB + b
                    if not first:
                        sp.wait_ge(ysum_done, n - NB + 1)
                    for s in range(TOPK):
                        sp.dma_start(YC[:, b, s, :, :], y_tiles[s, :, bass.ds(n * CG, CG), :]).then_inc(y_in[b], 16)

                run_out(sp, body)

            @block.vector
            def _(dve):
                def body(it, b, first):
                    n = it * NB + b
                    dve.wait_ge(y_in[b], 32 * (it + 1))
                    if not first:
                        dve.wait_ge(out_ready, n - NB + 1)
                    nc.vector.tensor_tensor(YSUM[:, b, :, :], YC[:, b, 0, :, :], YC[:, b, 1, :, :], ALU.add).then_inc(ysum_done, 1)
                    dve.wait_ge(ysum_done, n + 1)
                    here = X[:, bass.ds(n * CG, CG), :]
                    nc.vector.tensor_tensor(here, here, YSUM[:, b, :, :], ALU.add).then_inc(out_ready, 1)

                run_out(dve, body)

            @block.scalar
            def _(act):
                def body(it, b, first):
                    n = it * NB + b
                    act.wait_ge(out_ready, n + 1)
                    act.dma_start(out_tiles[:, bass.ds(n * CG, CG), :], X[:, bass.ds(n * CG, CG), :]).then_inc(stored, 16)

                run_out(act, body)
                act.wait_ge(stored, 16 * CSTEPS)


DVE_LINKS, POOL_LINKS = 23, 6

CONST_WIDTHS = (("ident", 128), ("hmask", HG), ("iota8", EXPERTS), ("base8", EXPERTS), ("tri8", EXPERTS * EXPERTS),
                ("iota_tiles", ETILES), ("tri", SEQ), ("rank", 128), ("ones", 128),
                ("centre", DIM))


def shape_constants(np):
    p = np.arange(128)
    tables = {
        "ident": np.eye(128),
        "hmask": (p[:, None] // DK) % HG == np.arange(HG)[None, :],
        "iota8": np.tile(np.arange(EXPERTS), (128, 1)),
        "base8": np.tile(np.arange(EXPERTS) * REGION, (128, 1)),
        "tri8": np.tile((np.arange(EXPERTS)[None, :] <= np.arange(EXPERTS)[:, None]).reshape(1, -1), (128, 1)),
        "iota_tiles": np.tile(np.arange(ETILES), (128, 1)),
        "tri": np.where(np.arange(SEQ)[None, :] > p[:, None] % SEQ, NEG, 0.0),
        "rank": p[:, None] < p[None, :],
        "ones": np.ones((128, 128)),
        "centre": np.eye(DIM) - 1.0 / DIM,
    }
    consts = np.concatenate([tables[n].astype(np.float32) for n, _ in CONST_WIDTHS], axis=1)
    dest = np.arange(TOPK)[None, :, None] * TOKENS + p[:, None, None] * TILES + np.arange(TILES)[None, None, :]
    pad = np.zeros((PADS * ETILE, ROW), np.float32)
    pad.view(np.int32)[:, DIM + 1] = TOPK * TOKENS + np.arange(PADS * ETILE)
    return consts, dest.astype(np.int32), pad


def kernel(**inputs):
    import numpy as np
    import concourse.bacc as bacc
    from concourse.bass_utils import run_bass_kernel_spmd

    def w(name):
        return np.asarray(inputs["L0_ffn_" + name])

    consts, dest, pad = shape_constants(np)
    experts = np.concatenate([w("w1").transpose(0, 2, 1), w("w3").transpose(0, 2, 1), w("w2").transpose(0, 2, 1),
                              w("b1")[:, :, None], w("b3")[:, :, None],
                              np.broadcast_to(w("b2")[:, None, :], (EXPERTS, 128, DIM))], axis=2).reshape(EXPERTS * 128, WROW)
    inputs_t = np.stack([np.asarray(inputs[n]).reshape(UNITS, UTOK, DIM) for n in ("x", "ctx_1024")], axis=1)
    inputs_t = inputs_t.transpose(3, 0, 1, 2).reshape(DIM, UNITS * 2 * UTOK)

    def on_rows(a):
        return np.broadcast_to(np.asarray(a).reshape(1, -1), (128, np.asarray(a).size))

    def by_partition(a):
        return a.reshape(SHARED // 128, 128, -1).transpose(1, 0, 2).reshape(128, -1)

    attention_w = np.concatenate([np.asarray(inputs["L0_xattn_" + n]) for n in ("WQ", "WK", "WV", "WO")]
                                 + [w("gate_w").T, on_rows(w("gate_b")), on_rows(inputs["g_xattn"]), on_rows(inputs["g_ffn"])], axis=1)
    shared_w = np.concatenate([w("ws1").T, w("ws3").T, by_partition(w("ws2").T), by_partition(w("bs1")), by_partition(w("bs3")),
                               on_rows(w("bs2"))], axis=1)
    arrays = {
        "x": inputs["x"], "inputs_t": inputs_t, "mask": inputs["mask_BxS2_ik0"], "attention_w": attention_w,
        "shared_w": shared_w, "experts": experts, "consts": consts, "dest_rows": dest, "pad_rows": pad,
    }
    nc = bacc.Bacc("TRN2", target_bir_lowering=False, num_devices=1)
    feed, args = {}, {}
    for name, a in arrays.items():
        a = np.ascontiguousarray(np.asarray(a))
        feed["in_" + name] = a
        args[name] = nc.dram_tensor("in_" + name, a.shape, mybir.dt.from_np(a.dtype), kind="ExternalInput").ap()
    args["out"] = nc.dram_tensor("out", (BATCH, SEQ, DIM), mybir.dt.float32, kind="ExternalOutput").ap()
    build_program(nc, **args)
    r = run_bass_kernel_spmd(nc, [feed], core_ids=[0])
    return r.results[0]["out"]
```
